# Optimizing a Trainium2 kernel written in Bass

```python
import numpy as np
import jax
import jax.numpy as jnp

def _softmax(x, axis=-1):
    return jax.nn.softmax(x, axis=axis)

def _gelu(x):
    return jax.nn.gelu(x, approximate=True)

def _silu(x):
    return jax.nn.silu(x)

def _sigmoid(x):
    return jax.nn.sigmoid(x)

def _layernorm(x, axis=-1, eps=1e-05):
    m = jnp.mean(x, axis=axis, keepdims=True)
    v = jnp.var(x, axis=axis, keepdims=True)
    return (x - m) / jnp.sqrt(v + eps)

def _scatter_add(tgt, idx, src, axis=0):
    return tgt.at[idx].add(src)

def _segment_sum(src, seg, n):
    return jax.ops.segment_sum(src, seg, n)
kernel_name = 'mk_gnn_resnorm_d4_gnn_r32_20a787'

def setup_inputs(seed: int=0):
    np.random.seed(seed)
    _w = jnp.asarray

    def _rec_inputs():
        import jax
        import jax.numpy as jnp
        _gk = jax.random.key(seed)
        x = 0.0002542 + 0.9999 * jax.random.normal(jax.random.fold_in(_gk, 1), (6250, 64), jnp.float32)
        src = jax.random.randint(jax.random.fold_in(_gk, 2), (100000,), 0, 6250, jnp.int32)
        dst = jax.random.randint(jax.random.fold_in(_gk, 3), (100000,), 0, 6250, jnp.int32)
        _o = jnp.argsort(dst, stable=True)
        src = src[_o]
        dst = dst[_o]
        edge_attr_32 = -9.77346e-05 + 0.999888 * jax.random.normal(jax.random.fold_in(_gk, 12), (100000, 32), jnp.float32)
        edge_type_2 = jax.random.randint(jax.random.fold_in(_gk, 14), (100000,), 0, 2, jnp.int32)
        return (x, src, dst, edge_attr_32, edge_type_2)
    x, src, dst, edge_attr_32, edge_type_2 = _rec_inputs()

    def _L0_gnn_setup():
        import jax, jax.numpy as jnp
        import numpy as np
        N_ENTITIES = 6250
        N_RELATIONS = 2
        EMBED_DIM = 64
        N_EDGES = 62500
        key = jax.random.key(seed)
        k1, k2, k3, k4, k5, k6, k7, k8 = jax.random.split(key, 8)
        edge_index = jax.random.randint(k1, (2, N_EDGES), 0, N_ENTITIES, dtype=jnp.int32)
        edge_type = jax.random.randint(k2, (N_EDGES,), 0, N_RELATIONS, dtype=jnp.int32)
        entity_emb = jax.random.normal(k3, (N_ENTITIES, EMBED_DIM), dtype=jnp.float32)
        relation_emb = jax.random.normal(k4, (N_RELATIONS, EMBED_DIM), dtype=jnp.float32)
        att_w = jax.random.normal(k5, (2 * EMBED_DIM, 1), dtype=jnp.float32) * 0.08
        att_b = jax.random.normal(k6, (1,), dtype=jnp.float32) * 0.08
        W_w = jax.random.normal(k7, (EMBED_DIM, EMBED_DIM), dtype=jnp.float32) * 0.12
        W_b = jax.random.normal(k8, (EMBED_DIM,), dtype=jnp.float32) * 0.12
        return {'edge_index': edge_index, 'edge_type': edge_type, 'entity_emb': entity_emb, 'relation_emb': relation_emb, 'att_w': att_w, 'att_b': att_b, 'W_w': W_w, 'W_b': W_b}
    _L0_gnn_all = _L0_gnn_setup()
    _L0_gnn_in = {k: v for k, v in _L0_gnn_all.items() if k in ('relation_emb', 'att_w', 'att_b', 'W_w', 'W_b')}
    del _L0_gnn_all

    def _L1_gnn_setup():
        import jax, jax.numpy as jnp
        import numpy as np
        N_NODES = 3125
        DIM = 64
        N_EDGES = 37500
        SLOPE = 0.2

        def _segment_softmax(logits, seg, n):
            m = jax.ops.segment_max(logits, seg, num_segments=n)
            e = jnp.exp(logits - m[seg])
            z = jax.ops.segment_sum(e, seg, num_segments=n)
            return e / z[seg]

        def _gat_layer(x, src, dst, W, a_src, a_dst, b, n):
            h = x @ W
            al = h @ a_src
            ar = h @ a_dst
            logit = jax.nn.leaky_relu(al[src] + ar[dst], SLOPE)
            alpha = _segment_softmax(logit, dst, n)
            out = jax.ops.segment_sum(alpha[:, None] * h[src], dst, num_segments=n)
            return out + b
        key = jax.random.key(seed)
        ks = jax.random.split(key, 10)
        s = 1.0 / np.sqrt(DIM)
        return {'x': jax.random.normal(ks[0], (N_NODES, DIM), jnp.float32), 'edge_index': jax.random.randint(ks[1], (2, N_EDGES), 0, N_NODES, jnp.int32), 'W_std': jax.random.normal(ks[2], (DIM, DIM), jnp.float32) * s, 'a_src_std': jax.random.normal(ks[3], (DIM,), jnp.float32) * s, 'a_dst_std': jax.random.normal(ks[4], (DIM,), jnp.float32) * s, 'b_std': jnp.zeros((DIM,), jnp.float32), 'W_skip': jax.random.normal(ks[5], (2 * DIM, DIM), jnp.float32) * (1.0 / np.sqrt(2 * DIM)), 'a_src_skip': jax.random.normal(ks[6], (DIM,), jnp.float32) * s, 'a_dst_skip': jax.random.normal(ks[7], (DIM,), jnp.float32) * s, 'b_skip': jnp.zeros((DIM,), jnp.float32)}
    _L1_gnn_all = _L1_gnn_setup()
    _L1_gnn_in = {k: v for k, v in _L1_gnn_all.items() if k in ('W_std', 'a_src_std', 'a_dst_std', 'b_std', 'W_skip', 'a_src_skip', 'a_dst_skip', 'b_skip')}
    del _L1_gnn_all

    def _L2_gnn_setup():
        import jax, jax.numpy as jnp
        import numpy as np
        N_NODES = 3125
        N_EDGES = 50000
        IN_FEATS = 64
        OUT_FEATS = 64
        NEG_SLOPE = 0.2
        key = jax.random.key(seed)
        ks = jax.random.split(key, 8)
        feat = jax.random.normal(ks[0], (N_NODES, IN_FEATS), dtype=jnp.float32)
        src = jax.random.randint(ks[1], (N_EDGES,), 0, N_NODES, dtype=jnp.int64 if jax.config.jax_enable_x64 else jnp.int32).astype(jnp.int32)
        dst = jax.random.randint(ks[2], (N_EDGES,), 0, N_NODES, dtype=jnp.int64 if jax.config.jax_enable_x64 else jnp.int32).astype(jnp.int32)
        scale = 1.0 / np.sqrt(IN_FEATS)
        Wq = jax.random.normal(ks[3], (IN_FEATS, OUT_FEATS), dtype=jnp.float32) * scale
        Wk = jax.random.normal(ks[4], (IN_FEATS, OUT_FEATS), dtype=jnp.float32) * scale
        Wf = jax.random.normal(ks[5], (IN_FEATS, OUT_FEATS), dtype=jnp.float32) * scale
        bq = jnp.zeros((OUT_FEATS,), dtype=jnp.float32)
        bk = jnp.zeros((OUT_FEATS,), dtype=jnp.float32)
        bf = jnp.zeros((OUT_FEATS,), dtype=jnp.float32)
        return {'feat': feat, 'src': src, 'dst': dst, 'Wq': Wq, 'bq': bq, 'Wk': Wk, 'bk': bk, 'Wf': Wf, 'bf': bf}
    _L2_gnn_all = _L2_gnn_setup()
    _L2_gnn_in = {k: v for k, v in _L2_gnn_all.items() if k in ('Wq', 'bq', 'Wk', 'bk', 'Wf', 'bf')}
    del _L2_gnn_all

    def _L3_gnn_setup():
        import jax, jax.numpy as jnp
        import numpy as np
        N = 50000
        E = 50000
        D = 64
        DE = 32
        H = 4
        L = 3

        def _ln(x, g, b):
            mu = x.mean(-1, keepdims=True)
            var = ((x - mu) ** 2).mean(-1, keepdims=True)
            return (x - mu) / jnp.sqrt(var + 1e-05) * g + b

        def _delta_forward(h, e, src, dst, Wq, Wk, Wv, Wo, We, Wem, bem, gn, bn, ge, be):
            n = h.shape[0]
            dh = D // H
            for i in range(L):
                q = (h @ Wq[i]).reshape(n, H, dh)
                k = (h @ Wk[i]).reshape(n, H, dh)
                v = (h @ Wv[i]).reshape(n, H, dh)
                scores = jnp.einsum('ehd,ehd->eh', q[dst], k[src]) / jnp.sqrt(jnp.float32(dh))
                scores = scores + e @ We[i]
                m = jax.ops.segment_max(scores, dst, num_segments=n)
                p = jnp.exp(scores - m[dst])
                denom = jax.ops.segment_sum(p, dst, num_segments=n)
                alpha = p / (denom[dst] + 1e-09)
                msg = (alpha[:, :, None] * v[src]).reshape(-1, D)
                agg = jax.ops.segment_sum(msg, dst, num_segments=n)
                h = _ln(h + agg @ Wo[i], gn[i], bn[i])
                emsg = jax.nn.gelu(jnp.concatenate([h[src], h[dst], e], axis=-1) @ Wem[i] + bem[i])
                e = _ln(e + emsg, ge[i], be[i])
            return h
        key = jax.random.key(seed)
        ks = jax.random.split(key, 16)
        s = 0.05
        return {'node_features': jax.random.normal(ks[0], (N, D), jnp.float32), 'edge_features': jax.random.normal(ks[1], (E, DE), jnp.float32), 'edge_index': jax.random.randint(ks[2], (2, E), 0, N), 'Wq': jax.random.normal(ks[3], (L, D, D), jnp.float32) * s, 'Wk': jax.random.normal(ks[4], (L, D, D), jnp.float32) * s, 'Wv': jax.random.normal(ks[5], (L, D, D), jnp.float32) * s, 'Wo': jax.random.normal(ks[6], (L, D, D), jnp.float32) * s, 'We': jax.random.normal(ks[7], (L, DE, H), jnp.float32) * s, 'Wem': jax.random.normal(ks[8], (L, 2 * D + DE, DE), jnp.float32) * s, 'bem': jnp.zeros((L, DE), jnp.float32), 'gn': jnp.ones((L, D), jnp.float32), 'bn': jnp.zeros((L, D), jnp.float32), 'ge': jnp.ones((L, DE), jnp.float32), 'be': jnp.zeros((L, DE), jnp.float32)}
    _L3_gnn_all = _L3_gnn_setup()
    _L3_gnn_in = {k: v for k, v in _L3_gnn_all.items() if k in ('Wq', 'Wk', 'Wv', 'Wo', 'We', 'Wem', 'bem', 'gn', 'bn', 'ge', 'be')}
    del _L3_gnn_all
    return {'x': x, 'src': src, 'dst': dst, 'edge_attr_32': edge_attr_32, 'edge_type_2': edge_type_2, 'L0_gnn_relation_emb': _L0_gnn_in['relation_emb'], 'L0_gnn_att_w': _L0_gnn_in['att_w'], 'L0_gnn_att_b': _L0_gnn_in['att_b'], 'L0_gnn_W_w': _L0_gnn_in['W_w'], 'L0_gnn_W_b': _L0_gnn_in['W_b'], 'L1_gnn_W_std': _L1_gnn_in['W_std'], 'L1_gnn_a_src_std': _L1_gnn_in['a_src_std'], 'L1_gnn_a_dst_std': _L1_gnn_in['a_dst_std'], 'L1_gnn_b_std': _L1_gnn_in['b_std'], 'L1_gnn_W_skip': _L1_gnn_in['W_skip'], 'L1_gnn_a_src_skip': _L1_gnn_in['a_src_skip'], 'L1_gnn_a_dst_skip': _L1_gnn_in['a_dst_skip'], 'L1_gnn_b_skip': _L1_gnn_in['b_skip'], 'L2_gnn_Wq': _L2_gnn_in['Wq'], 'L2_gnn_bq': _L2_gnn_in['bq'], 'L2_gnn_Wk': _L2_gnn_in['Wk'], 'L2_gnn_bk': _L2_gnn_in['bk'], 'L2_gnn_Wf': _L2_gnn_in['Wf'], 'L2_gnn_bf': _L2_gnn_in['bf'], 'L3_gnn_Wq': _L3_gnn_in['Wq'], 'L3_gnn_Wk': _L3_gnn_in['Wk'], 'L3_gnn_Wv': _L3_gnn_in['Wv'], 'L3_gnn_Wo': _L3_gnn_in['Wo'], 'L3_gnn_We': _L3_gnn_in['We'], 'L3_gnn_Wem': _L3_gnn_in['Wem'], 'L3_gnn_bem': _L3_gnn_in['bem'], 'L3_gnn_gn': _L3_gnn_in['gn'], 'L3_gnn_bn': _L3_gnn_in['bn'], 'L3_gnn_ge': _L3_gnn_in['ge'], 'L3_gnn_be': _L3_gnn_in['be']}

def reference(x, src, dst, edge_attr_32, edge_type_2, L0_gnn_relation_emb, L0_gnn_att_w, L0_gnn_att_b, L0_gnn_W_w, L0_gnn_W_b, L1_gnn_W_std, L1_gnn_a_src_std, L1_gnn_a_dst_std, L1_gnn_b_std, L1_gnn_W_skip, L1_gnn_a_src_skip, L1_gnn_a_dst_skip, L1_gnn_b_skip, L2_gnn_Wq, L2_gnn_bq, L2_gnn_Wk, L2_gnn_bk, L2_gnn_Wf, L2_gnn_bf, L3_gnn_Wq, L3_gnn_Wk, L3_gnn_Wv, L3_gnn_Wo, L3_gnn_We, L3_gnn_Wem, L3_gnn_bem, L3_gnn_gn, L3_gnn_bn, L3_gnn_ge, L3_gnn_be):
    import jax
    import jax.numpy as jnp

    def _L0_gnn_ref(edge_index, edge_type, entity_emb, relation_emb, att_w, att_b, W_w, W_b):
        import jax, jax.numpy as jnp
        import numpy as np
        N_ENTITIES = 6250
        N_RELATIONS = 2
        EMBED_DIM = 64
        N_EDGES = 62500
        head = entity_emb[edge_index[0]]
        tail = entity_emb[edge_index[1]]
        rel = relation_emb[edge_type]
        head_rel = jnp.concatenate([head, rel], axis=-1)
        att_scores = jax.nn.sigmoid(head_rel @ att_w + att_b)
        neighbor_emb = att_scores * tail
        aggr_emb = jax.ops.segment_sum(neighbor_emb, edge_index[0], num_segments=N_ENTITIES)
        return jnp.tanh(aggr_emb @ W_w.T + W_b)

    def _L1_gnn_ref(x, edge_index, W_std, a_src_std, a_dst_std, b_std, W_skip, a_src_skip, a_dst_skip, b_skip):
        import jax, jax.numpy as jnp
        import numpy as np
        N_NODES = 3125
        DIM = 64
        N_EDGES = 37500
        SLOPE = 0.2

        def _segment_softmax(logits, seg, n):
            m = jax.ops.segment_max(logits, seg, num_segments=n)
            e = jnp.exp(logits - m[seg])
            z = jax.ops.segment_sum(e, seg, num_segments=n)
            return e / z[seg]

        def _gat_layer(x, src, dst, W, a_src, a_dst, b, n):
            h = x @ W
            al = h @ a_src
            ar = h @ a_dst
            logit = jax.nn.leaky_relu(al[src] + ar[dst], SLOPE)
            alpha = _segment_softmax(logit, dst, n)
            out = jax.ops.segment_sum(alpha[:, None] * h[src], dst, num_segments=n)
            return out + b
        n = x.shape[0]
        loops = jnp.arange(n, dtype=edge_index.dtype)
        src = jnp.concatenate([edge_index[0], loops])
        dst = jnp.concatenate([edge_index[1], loops])
        in_x = x
        for _ in range(4):
            x = _gat_layer(x, src, dst, W_std, a_src_std, a_dst_std, b_std, n)
            x = jax.nn.gelu(x, approximate=False)
        xcat = jnp.concatenate([in_x, x], axis=1)
        return _gat_layer(xcat, src, dst, W_skip, a_src_skip, a_dst_skip, b_skip, n)

    def _L2_gnn_ref(feat, src, dst, Wq, bq, Wk, bk, Wf, bf):
        import jax, jax.numpy as jnp
        import numpy as np
        N_NODES = 3125
        N_EDGES = 50000
        IN_FEATS = 64
        OUT_FEATS = 64
        NEG_SLOPE = 0.2
        N = feat.shape[0]
        q = feat @ Wq + bq
        k = feat @ Wk + bk
        f = feat @ Wf + bf
        e = jnp.sum(k[src] * q[dst], axis=-1)
        e = jax.nn.leaky_relu(e, negative_slope=NEG_SLOPE)
        emax = jax.ops.segment_max(e, dst, num_segments=N)
        emax = jnp.where(jnp.isfinite(emax), emax, 0.0)
        ez = jnp.exp(e - emax[dst])
        denom = jax.ops.segment_sum(ez, dst, num_segments=N)
        a = ez / denom[dst]
        out = jax.ops.segment_sum(f[src] * a[:, None], dst, num_segments=N)
        return out

    def _L3_gnn_ref(node_features, edge_features, edge_index, Wq, Wk, Wv, Wo, We, Wem, bem, gn, bn, ge, be):
        import jax, jax.numpy as jnp
        import numpy as np
        N = 50000
        E = 50000
        D = 64
        DE = 32
        H = 4
        L = 3

        def _ln(x, g, b):
            mu = x.mean(-1, keepdims=True)
            var = ((x - mu) ** 2).mean(-1, keepdims=True)
            return (x - mu) / jnp.sqrt(var + 1e-05) * g + b

        def _delta_forward(h, e, src, dst, Wq, Wk, Wv, Wo, We, Wem, bem, gn, bn, ge, be):
            n = h.shape[0]
            dh = D // H
            for i in range(L):
                q = (h @ Wq[i]).reshape(n, H, dh)
                k = (h @ Wk[i]).reshape(n, H, dh)
                v = (h @ Wv[i]).reshape(n, H, dh)
                scores = jnp.einsum('ehd,ehd->eh', q[dst], k[src]) / jnp.sqrt(jnp.float32(dh))
                scores = scores + e @ We[i]
                m = jax.ops.segment_max(scores, dst, num_segments=n)
                p = jnp.exp(scores - m[dst])
                denom = jax.ops.segment_sum(p, dst, num_segments=n)
                alpha = p / (denom[dst] + 1e-09)
                msg = (alpha[:, :, None] * v[src]).reshape(-1, D)
                agg = jax.ops.segment_sum(msg, dst, num_segments=n)
                h = _ln(h + agg @ Wo[i], gn[i], bn[i])
                emsg = jax.nn.gelu(jnp.concatenate([h[src], h[dst], e], axis=-1) @ Wem[i] + bem[i])
                e = _ln(e + emsg, ge[i], be[i])
            return h
        src = edge_index[0]
        dst = edge_index[1]
        return _delta_forward(node_features, edge_features, src, dst, Wq, Wk, Wv, Wo, We, Wem, bem, gn, bn, ge, be)
    edge_index = jnp.stack([src, dst])
    x = _layernorm(x + _L0_gnn_ref(edge_index, edge_type_2, x, L0_gnn_relation_emb, L0_gnn_att_w, L0_gnn_att_b, L0_gnn_W_w, L0_gnn_W_b), axis=-1)
    x = _layernorm(x + _L1_gnn_ref(x, edge_index, L1_gnn_W_std, L1_gnn_a_src_std, L1_gnn_a_dst_std, L1_gnn_b_std, L1_gnn_W_skip, L1_gnn_a_src_skip, L1_gnn_a_dst_skip, L1_gnn_b_skip), axis=-1)
    x = _layernorm(x + _L2_gnn_ref(x, src, dst, L2_gnn_Wq, L2_gnn_bq, L2_gnn_Wk, L2_gnn_bk, L2_gnn_Wf, L2_gnn_bf), axis=-1)
    x = _layernorm(x + _L3_gnn_ref(x, edge_attr_32, edge_index, L3_gnn_Wq, L3_gnn_Wk, L3_gnn_Wv, L3_gnn_Wo, L3_gnn_We, L3_gnn_Wem, L3_gnn_bem, L3_gnn_gn, L3_gnn_bn, L3_gnn_ge, L3_gnn_be), axis=-1)
    return x

_drawn_inputs = setup_inputs


def setup_inputs(seed=0):
    import zlib

    import numpy as np

    out = dict(_drawn_inputs(seed))
    spreads = {'L1_gnn_b_std': (0.0, 0.1),
     'L1_gnn_b_skip': (0.0, 0.1),
     'L2_gnn_bq': (0.0, 0.1),
     'L2_gnn_bk': (0.0, 0.8),
     'L2_gnn_bf': (0.0, 0.1),
     'L3_gnn_bem': (0.0, 2.0),
     'L3_gnn_gn': (1.0, 0.2),
     'L3_gnn_bn': (0.0, 0.1),
     'L3_gnn_ge': (1.0, 0.6),
     'L3_gnn_be': (0.0, 2.0)}
    factors = {'edge_attr_32': 5.617,
     'L1_gnn_a_src_std': 5.56,
     'L1_gnn_a_dst_std': 167.698,
     'L3_gnn_Wq': 8.0,
     'L3_gnn_Wk': 8.0,
     'L3_gnn_We': 5.39,
     'L3_gnn_Wem': 8.0}
    for name, (base, spread) in spreads.items():
        noise = np.random.default_rng([zlib.crc32(name.encode()), seed]).standard_normal(out[name].shape)
        drawn = base * np.exp(spread * noise) if base else spread * noise
        out[name] = jnp.asarray(drawn.astype(out[name].dtype))
    for name, factor in factors.items():
        out[name] = (out[name] * factor).astype(out[name].dtype)
    return out
```

```python
from contextlib import ExitStack, contextmanager

import numpy as np
import concourse.bass as bass
from concourse import mybir

F32 = mybir.dt.float32
I32 = mybir.dt.int32
BF16 = mybir.dt.bfloat16
ALU = mybir.AluOpType
ACT = mybir.ActivationFunctionType
AX = mybir.AxisListType

P = 128
N, E, D, DE, NH = 6250, 100000, 64, 32, 4
C = -(-N // P)
NP = P * C
K = 28
CHUNKS = 28
KT = K * CHUNKS
EP = P * KT
LOOPS = CHUNKS // 2
BIG = 1.0e30
REP = 4
ACC_ROWS = 2 * NP + P
E_ROWS = EP + 1 + P
B_ROWS = EP + NP
assert EP >= E and NP > N and KT % K == 0


class Link:

    def __init__(self, eng, sem, base=0):
        self.eng, self.sem, self.base, self.n = eng, sem, base, 0

    def __call__(self, ins):
        self.n += 1
        ins.then_inc(self.sem, 1)
        self.eng.wait_ge(self.sem, self.base + self.n)


def scratch(nc, name, shape, dtype=F32):
    return nc.sbuf_tensor(f"{name}_{nc.next_id()}", shape, dtype)


class Phase(dict):

    def __init__(self, nc, names, pairs, ctx):
        self.nc, self.ctx, self.opened = nc, ctx, ExitStack()
        self.sems = []
        for n in names.split():
            self.sems.append(ctx.enter_context(nc.semaphore(n)))
            self[n] = self.sems[-1]
        for n in pairs.split():
            two = [ctx.enter_context(nc.semaphore(f"{n}{i}")) for i in range(2)]
            self.sems += two
            self[n] = two

    def sbuf(self, name, shape, dtype=F32):
        return self.ctx.enter_context(scratch(self.nc, name, shape, dtype))

    def psum(self, name, shape):
        return self.ctx.enter_context(self.nc.psum_tensor(f"{name}_{self.nc.next_id()}", shape, F32))

    def block(self):
        return self.opened.enter_context(self.nc.Block())


@contextmanager
def phase(nc, names, pairs=""):
    with ExitStack() as ctx:
        s = Phase(nc, names, pairs, ctx)
        with s.opened:
            yield s
        with nc.Block() as block:
            @block.gpsimd
            def _(gp):
                gp.dma_reset()
                for h in s.sems:
                    gp.sem_clear(h)


def node_rows(dram):
    return dram.rearrange("(c p) w -> p c w", p=P)


def edge_rows(dram):
    return dram[0:EP, :].rearrange("(p k) w -> p k w", p=P)


def edge_rows_after(dram, n):
    return dram[n:EP + n, :].rearrange("(p k) w -> p k w", p=P)


def offset(ap):
    return bass.IndirectOffsetOnAxis(ap=ap, axis=0)


def bc(ap, n):
    return ap.unsqueeze(len(ap.shape)).to_broadcast([*ap.shape, n])


def mid(ap, n):
    return ap.unsqueeze(1).to_broadcast([ap.shape[0], n, ap.shape[1]])


def flat(ap):
    return ap.rearrange("p a b -> p (a b)")


def prepare(nc, g, a):
    with phase(nc, "loaded hist_done dve_link pool_link pe_done zeros_set zeroed ready stored", "onehot_ready onehot_used") as s:
        dst_i = s.sbuf("dst_i", [P, KT + 2], I32)
        dst_f = s.sbuf("dst_f", [P, KT + 2])
        lo_i = s.sbuf("lo_i", [P, KT], I32)
        lo_f = s.sbuf("lo_f", [P, KT])
        hi_f = s.sbuf("hi_f", [P, KT])
        typ_i = s.sbuf("typ_i", [P, KT], I32)
        key_i = s.sbuf("key_i", [P, KT], I32)
        work = s.sbuf("work", [P, KT])
        kpos = s.sbuf("kpos", [P, KT], I32)
        iota_i = s.sbuf("iota_i", [P, P], I32)
        pcol_i = s.sbuf("pcol_i", [P, 1], I32)
        ncol_i = s.sbuf("ncol_i", [P, C], I32)
        ncol = s.sbuf("ncol", [P, C])
        lo_hot = s.sbuf("lo_hot", [P, 2, K, P], BF16)
        hi_hot = s.sbuf("hi_hot", [P, 2, K, C], BF16)
        zero_hot = s.sbuf("zero_hot", [P, P], BF16)
        zeros = s.sbuf("zeros", [P, 1568])
        empty = s.sbuf("empty", [1, 72])
        count = s.sbuf("count", [P, C])
        nonempty = s.sbuf("nonempty", [P, C])
        sums = s.sbuf("sums", [P, 4, C])
        bnd = s.sbuf("bnd", [P, 8])
        gat_wT = s.sbuf("gat_wT", [D, D + 2 * D])
        gat_a = s.sbuf("gat_a", [D, 4])
        ps_hist = s.psum("ps_hist", [P, 512])
        ps_cum = s.psum("ps_cum", [P, 512])
        ps_tot = s.psum("ps_tot", [P, 512])
        ps_w = s.psum("ps_w", [P, 512])
        block = s.block()
        LOADS = 6

        @block.sync
        def _(sp):
            sp.dma_start(dst_i[:], a["dst_ext"]).then_inc(s["loaded"], 16)
            sp.dma_start(g.src[:, 0:KT], a["src_pad"]).then_inc(s["loaded"], 16)
            sp.dma_start(typ_i[:], a["type_pad"]).then_inc(s["loaded"], 16)
            sp.dma_start(g.x[:], node_rows(a["x_pad"])).then_inc(s["loaded"], 16)
            sp.dma_start(gat_wT[:], a["gat_wT"]).then_inc(s["loaded"], 16)
            sp.dma_start(gat_a[:], a["gat_a"]).then_inc(s["loaded"], 16)
            sp.dma_start(g.gat_w[:, 0, 0:D], a["gat_w_skip"]).then_inc(s["loaded"], 16)
            sp.dma_start(g.gat_w[0:D, 1, 0:D], a["gat_w_std"]).then_inc(s["loaded"], 16)
            sp.wait_ge(s["ready"], 1)
            sp.dma_start(g.d_key[:, :], key_i[:]).then_inc(s["stored"], 16)
            sp.wait_ge(s["stored"], 16)
            sp.wait_ge(s["loaded"], 16 * (LOADS + 2))

        @block.scalar
        def _(act):
            act.wait_ge(s["zeros_set"], 1)
            act.wait_ge(s["loaded"], 16 * (LOADS + 2))
            act.dma_start(g.d_b64[0:EP, :].rearrange("(p k) w -> p (k w)", p=P).rearrange("p (r x) -> p r x", x=1568),
                          mid(zeros[:], KT * D // 1568)).then_inc(s["zeroed"], 16)
            n = 1
            for r in range(REP):
                act.dma_start(g.d_acc[r][0:2 * NP, :].rearrange("(p k) w -> p (k w)", p=P)
                              .rearrange("p (r x) -> p r x", x=1568),
                              mid(zeros[:], 2 * C * D // 1568)).then_inc(s["zeroed"], 16)
                act.dma_start(g.d_acc[r][2 * NP:, :], zeros[:, 0:D]).then_inc(s["zeroed"], 16)
                n += 2
            for d in (g.d_b1, g.d_b64, g.d_b96):
                act.dma_start(d[EP:EP + 2 * K, :], zeros[0:2 * K, 0:d.shape[1]]).then_inc(s["zeroed"], 16)
                n += 1
            for d in (g.d_e66, g.d_e72):
                w = d.shape[1]
                act.dma_start(d[EP + 1:, :], zeros[:, 0:w]).then_inc(s["zeroed"], 16)
                act.dma_start(d[EP:EP + 1, 0:w], empty[0:1, 72 - w:72]).then_inc(s["zeroed"], 16)
                n += 2
            act.wait_ge(s["zeroed"], 16 * n)

        @block.gpsimd
        def _(gp):
            gp.iota(iota_i[:], [[1, P]], base=0, channel_multiplier=0).then_inc(s["pool_link"], 1)
            gp.iota(pcol_i[:], [[0, 1]], base=0, channel_multiplier=1).then_inc(s["pool_link"], 1)
            gp.iota(kpos[:], [[1, KT]], base=0, channel_multiplier=KT).then_inc(s["pool_link"], 1)
            gp.iota(ncol_i[:], [[P, C]], base=0, channel_multiplier=1).then_inc(s["pool_link"], 1)

        @block.vector
        def _(v):
            link = Link(v, s["dve_link"])
            link(nc.vector.memset(empty[:], 0.0))
            link(nc.vector.memset(empty[0:1, 68:72], -BIG))
            nc.vector.memset(zeros[:], 0.0).then_inc(s["zeros_set"], 1)
            link(nc.vector.memset(zero_hot[:], 0.0))
            link(nc.vector.memset(g.ones[:], 1.0))
            v.wait_ge(s["pool_link"], 4)
            link(nc.vector.tensor_copy(g.iota[:], iota_i[:]))
            link(nc.vector.tensor_copy(g.pcol[:], pcol_i[:]))
            link(nc.vector.tensor_copy(ncol[:], ncol_i[:]))
            link(nc.vector.tensor_scalar(g.ident[:], g.iota[:], g.pcol[:, 0:1], None, ALU.is_equal))
            link(nc.vector.tensor_scalar(g.before[:], g.iota[:], g.pcol[:, 0:1], None, ALU.is_gt))
            link(nc.vector.tensor_scalar(g.after[:], g.iota[:], g.pcol[:, 0:1], None, ALU.is_lt))
            v.wait_ge(s["loaded"], 16 * (LOADS + 2))
            link(nc.vector.tensor_copy(dst_f[:], dst_i[:]))
            link(nc.vector.tensor_tensor(g.same[:, 0:KT], dst_f[:, 1:KT + 1], dst_f[:, 0:KT], ALU.is_equal))
            link(nc.vector.memset(g.same[:, KT:], 0.0))
            link(nc.vector.memset(g.src[:, KT:], 0))
            link(nc.vector.tensor_scalar(g.cut[:], g.same[:, 0:KT], -1.0, BIG, ALU.add, ALU.mult))
            link(nc.vector.tensor_copy(g.dst0[:], dst_i[:, 1:2]))
            link(nc.vector.tensor_scalar(key_i[:], typ_i[:], float(NP), None, ALU.mult))
            nc.vector.tensor_tensor(key_i[:], key_i[:], g.src[:, 0:KT], ALU.add).then_inc(s["ready"], 1)
            link(nc.vector.tensor_scalar(lo_i[:], dst_i[:, 1:KT + 1], P - 1, None, ALU.bitwise_and))
            link(nc.vector.tensor_copy(lo_f[:], lo_i[:]))
            link(nc.vector.tensor_tensor(hi_f[:], dst_f[:, 1:KT + 1], lo_f[:], ALU.subtract))
            link(nc.vector.tensor_scalar(hi_f[:], hi_f[:], 1.0 / P, None, ALU.mult))
            link(nc.vector.tensor_tensor(work[:], dst_f[:, 2:KT + 2], dst_f[:, 1:KT + 1], ALU.is_equal))
            link(nc.vector.scalar_tensor_tensor(work[:], work[:], 4.0 * EP, kpos[:], ALU.mult, ALU.add))
            link(nc.vector.tensor_reduce(bnd[:, 0:1], work[:], AX.X, ALU.min))
            link(nc.vector.tensor_scalar(bnd[:, 1:2], bnd[:, 0:1], 2.0 * EP, None, ALU.is_lt))
            link(nc.vector.tensor_tensor(bnd[:, 1:2], bnd[:, 1:2], g.same[:, 0:1], ALU.mult))
            link(nc.vector.tensor_scalar(bnd[:, 2:3], g.pcol[:], float(EP + 1), None, ALU.add))
            link(nc.vector.tensor_tensor(bnd[:, 3:4], bnd[:, 0:1], bnd[:, 2:3], ALU.subtract))
            link(nc.vector.tensor_tensor(bnd[:, 3:4], bnd[:, 3:4], bnd[:, 1:2], ALU.mult))
            link(nc.vector.tensor_tensor(bnd[:, 3:4], bnd[:, 3:4], bnd[:, 2:3], ALU.add))
            link(nc.vector.tensor_copy(g.idx_join[:], bnd[:, 3:4]))
            link(nc.vector.tensor_reduce(bnd[:, 4:5], g.same[:, 0:KT], AX.X, ALU.min))
            link(nc.vector.tensor_scalar(bnd[:, 5:6], bnd[:, 4:5], -1.0, BIG, ALU.add, ALU.mult))
            with v.Fori(0, LOOPS) as t:
                for b in range(2):
                    cols = bass.ds((2 * t + b) * K, K)
                    v.wait_ge(s["onehot_used"][b], t + 1)
                    nc.vector.tensor_tensor(lo_hot[:, b], mid(g.iota[:], K), bc(lo_f[:, cols], P), ALU.is_equal)
                    nc.vector.tensor_tensor(hi_hot[:, b], mid(g.iota[:, 0:C], K), bc(hi_f[:, cols], C),
                                            ALU.is_equal).then_inc(s["onehot_ready"][b], 1)
            v.wait_ge(s["hist_done"], 1)
            link(nc.vector.tensor_copy(count[:], ps_hist[:, 0:C]))
            nc.vector.tensor_copy(sums[:, 0], count[:]).then_inc(s["ready"], 1)
            link(nc.vector.tensor_scalar(nonempty[:], count[:], 0.0, None, ALU.is_gt))
            v.wait_ge(s["pe_done"], 1)
            link(nc.vector.tensor_copy(sums[:, 1], ps_tot[:, 0:C]))
            link(nc.vector.tensor_tensor_scan(sums[:, 2], g.ones[:, 0:C], sums[:, 1], 0.0,
                                              ALU.mult, ALU.add))
            link(nc.vector.tensor_tensor(sums[:, 2], sums[:, 2], sums[:, 1], ALU.subtract))
            link(nc.vector.tensor_tensor(sums[:, 3], sums[:, 2], ps_cum[:, 0:C], ALU.add))
            link(nc.vector.tensor_tensor(sums[:, 1], sums[:, 3], count[:], ALU.add))
            link(nc.vector.tensor_scalar(sums[:, 1], sums[:, 1], -1.0 - EP, None, ALU.add))
            link(nc.vector.tensor_tensor(sums[:, 1], sums[:, 1], nonempty[:], ALU.mult))
            link(nc.vector.tensor_scalar(sums[:, 1], sums[:, 1], float(EP), None, ALU.add))
            link(nc.vector.tensor_copy(g.idx_last[:], sums[:, 1]))
            link(nc.vector.tensor_scalar(ncol[:], ncol[:], float(EP), None, ALU.add))
            link(nc.vector.tensor_tensor(sums[:, 3], sums[:, 3], ncol[:], ALU.subtract))
            link(nc.vector.tensor_tensor(sums[:, 3], sums[:, 3], nonempty[:], ALU.mult))
            link(nc.vector.tensor_tensor(sums[:, 3], sums[:, 3], ncol[:], ALU.add))
            link(nc.vector.tensor_copy(g.idx_first[:], sums[:, 3]))
            v.wait_ge(s["pe_done"], 2)
            link(nc.vector.tensor_copy(g.pass_cut[:], ps_tot[0:68, 128:256]))
            link(nc.vector.tensor_copy(g.gat_w[:, 0, D:D + 2], ps_w[:, 0:2]))
            link(nc.vector.tensor_copy(g.gat_w[0:D, 1, D:D + 2], ps_w[0:D, 2:4]))

        @block.tensor
        def _(pe):
            for b in range(2):
                pe.sem_inc(s["onehot_used"][b], 1)
            pe.wait_ge(s["dve_link"], 4)
            nc.tensor.matmul(ps_hist[:, 0:C], zero_hot[:], zero_hot[:, 0:C], start=True, stop=False)
            with pe.Fori(0, LOOPS) as t:
                for b in range(2):
                    pe.wait_ge(s["onehot_ready"][b], t + 1)
                    for k in range(K):
                        mm = nc.tensor.matmul(ps_hist[:, 0:C], lo_hot[:, b, k], hi_hot[:, b, k],
                                              start=False, stop=False)
                    mm.then_inc(s["onehot_used"][b], 1)
            nc.tensor.matmul(ps_hist[:, 0:C], zero_hot[:], zero_hot[:, 0:C],
                             start=False, stop=True).then_inc(s["hist_done"], 1)
            pe.wait_ge(s["ready"], 2)
            nc.tensor.matmul(ps_cum[:, 0:C], g.before[:], sums[:, 0], start=True, stop=True)
            nc.tensor.matmul(ps_tot[:, 0:C], g.ones[:], sums[:, 0], start=True, stop=True)
            nc.tensor.matmul(ps_tot[0:68, 128:256], bnd[:, 5:6].to_broadcast([P, 68]), g.ident[:],
                             start=True, stop=True).then_inc(s["pe_done"], 1)
            nc.tensor.matmul(ps_w[:, 0:2], gat_wT[:, 0:2 * D], gat_a[:, 0:2], start=True, stop=True)
            nc.tensor.matmul(ps_w[0:D, 2:4], gat_wT[:, 2 * D:], gat_a[:, 2:4],
                             start=True, stop=True).then_inc(s["pe_done"], 1)


def project(nc, g, rows, width, weights, extra, out_w, out, table=None, spread=None, seed=None,
            from_sbuf=False):
    kin = width + (1 if extra else 0)
    per = 512 // out_w
    groups = [(c0, min(c0 + per, C)) for c0 in range(0, C, per)]
    T4 = [(c0, min(c0 + 4, C)) for c0 in range(0, C, 4)]
    tables = [table] if table else []
    if seed is not None and seed[0] is not table[0]:
        tables.append((seed[0], *seed[1]))
    with phase(nc, "w_loaded ones_set turned turn_copied multiplied result_copied tabled spread_done seeded") as s:
        rows_T = s.sbuf("rows_T", [kin, C, P])
        w_sb = s.sbuf("w_sb", [kin, out_w])
        ps_turn0 = s.psum("ps_turn0", [P, 512])
        ps_turn1 = s.psum("ps_turn1", [P, 512])
        ps_out0 = s.psum("ps_out0", [P, 512])
        ps_out1 = s.psum("ps_out1", [P, 512])
        block = s.block()
        ps_turn, ps_out = (ps_turn0, ps_turn1), (ps_out0, ps_out1)

        @block.sync
        def _(sp):
            if not from_sbuf:
                sp.dma_start(w_sb[:], weights).then_inc(s["w_loaded"], 16)
            if table is not None:
                sp.wait_ge(s["result_copied"], len(groups))
                for d, c0, c1 in tables:
                    sp.dma_start(node_rows(d), out[:, :, c0:c1]).then_inc(s["tabled"], 16)
                sp.wait_ge(s["tabled"], 16 * len(tables))

        @block.tensor
        def _(pe):
            w = weights if from_sbuf else w_sb[:]
            if not from_sbuf:
                pe.wait_ge(s["w_loaded"], 16)
            if extra:
                pe.wait_ge(s["ones_set"], 1)

            def turn(i):
                c0, c1 = T4[i]
                if i >= 2:
                    pe.wait_ge(s["turn_copied"], i - 1)
                for c in range(c0, c1):
                    mm = nc.tensor.transpose(ps_turn[i % 2][0:width, (c - c0) * P:(c - c0 + 1) * P],
                                             rows[:, c, :], g.ident[:])
                mm.then_inc(s["turned"], 1)

            turns = 0
            for i, (c0, c1) in enumerate(groups):
                while turns < len(T4) and T4[turns][0] < min(c1 + 4, C):
                    turn(turns)
                    turns += 1
                pe.wait_ge(s["turn_copied"], (c1 - 1) // 4 + 1)
                if i >= 2:
                    pe.wait_ge(s["result_copied"], i - 1)
                for c in range(c0, c1):
                    mm = nc.tensor.matmul(ps_out[i % 2][:, (c - c0) * out_w:(c - c0 + 1) * out_w],
                                          rows_T[:, c, :], w, start=True, stop=True)
                mm.then_inc(s["multiplied"], 1)

        @block.scalar
        def _(act):
            for i, (c0, c1) in enumerate(T4):
                act.wait_ge(s["turned"], i + 1)
                nc.scalar.copy(flat(rows_T[0:width, c0:c1, :]),
                               ps_turn[i % 2][0:width, 0:(c1 - c0) * P]).then_inc(s["turn_copied"], 1)

        @block.vector
        def _(v):
            if extra:
                nc.vector.memset(rows_T[width:width + 1, :, :], 1.0).then_inc(s["ones_set"], 1)
            for i, (c0, c1) in enumerate(groups):
                v.wait_ge(s["multiplied"], i + 1)
                nc.vector.tensor_copy(out[:, c0:c1, 0:out_w],
                                      ps_out[i % 2][:, 0:(c1 - c0) * out_w].rearrange("p (c w) -> p c w", w=out_w)
                                      ).then_inc(s["result_copied"], 1)

        if spread is not None:
            @block.gpsimd
            def _(gp):
                d, c0, c1 = spread
                for i, (g0, g1) in enumerate(groups):
                    gp.wait_ge(s["result_copied"], i + 1)
                    for c in range(g0, g1):
                        gp.indirect_dma_start(d[:, :], offset(g.idx_first[:, c:c + 1]),
                                              out[:, c, c0:c1], None).then_inc(s["spread_done"], 16)
                gp.wait_ge(s["tabled"], 16 * len(tables))
                gp.indirect_dma_start(seed[2], None, seed[0][:, :], offset(g.dst0[:])).then_inc(s["seeded"], 16)
                gp.wait_ge(s["spread_done"], 16 * C)
                gp.wait_ge(s["seeded"], 16)


def spread_x(nc, g):
    with phase(nc, "spread_done seeded") as s:
        block = s.block()
        @block.gpsimd
        def _(gp):
            gp.indirect_dma_start(g.seed[:, 0:D], None, g.d_x[:, :], offset(g.dst0[:])).then_inc(s["seeded"], 16)
            for c in range(C):
                gp.indirect_dma_start(g.d_b64[:, :], offset(g.idx_first[:, c:c + 1]),
                                      g.x[:, c, :], None).then_inc(s["spread_done"], 16)
            gp.wait_ge(s["spread_done"], 16 * C)
            gp.wait_ge(s["seeded"], 16)


def layer0_edges(nc, g):
    BANK = 8
    SG = [(k, min(k + BANK, K)) for k in range(0, K, BANK)]
    KG = [(k, k + 4) for k in range(0, K, 4)]
    SG_BANKS = len(SG)
    with phase(nc, "pool_steps spread_link dve_link keys_f keys_turned pairs_ready rows_summed sums_copied "
               "wide_zeroed zeros_set",
               "b_loaded key_loaded spread_done added0 added1 added2 added3 idx_ready pairs_used") as s:
        b_x = s.sbuf("b_x", [P, 2, K, D])
        key = s.sbuf("key", [P, 2, K], I32)
        key_f = s.sbuf("key_f", [P, 2, K])
        same_c = s.sbuf("same_c", [P, K])
        pairs = s.sbuf("pairs", [P, 2, K, P])
        earlier = s.sbuf("earlier", [P, K, P])
        again = s.sbuf("again", [P, K])
        idx_f = s.sbuf("idx_f", [P, K])
        idx = s.sbuf("idx", [P, 2, K], I32)
        sums = s.sbuf("sums", [P, 2, K, D])
        spare = s.sbuf("spare", [P, 1])
        zeros = s.sbuf("zeros", [P, 2352])
        prime = s.sbuf("prime", [1, 2 * REP])
        ps_key0 = s.psum("ps_key0", [P, 512])
        ps_key1 = s.psum("ps_key1", [P, 512])
        ps_sum = s.psum("ps_sum", [P, SG_BANKS, 512])
        block = s.block()
        ps_key = (ps_key0, ps_key1)
        added = list(zip(s["added0"], s["added1"], s["added2"], s["added3"]))
        PER = K // REP
        LINKS = 6

        @block.sync
        def _(sp):
            with sp.Fori(0, LOOPS) as t:
                for b in range(2):
                    cols = bass.ds((2 * t + b) * K, K)
                    sp.wait_ge(s["pairs_used"][b], t + 1)
                    sp.dma_start(b_x[:, b], edge_rows(g.d_b64)[:, cols, :]).then_inc(s["b_loaded"][b], 16)
                    sp.dma_start(key[:, b], g.d_key[:, cols]).then_inc(s["key_loaded"][b], 16)

        @block.vector
        def _(v):
            nc.vector.memset(zeros[:], 0.0).then_inc(s["zeros_set"], 1)
            nc.vector.tensor_scalar(spare[:], g.pcol[:], float(2 * NP), None, ALU.add).then_inc(s["spread_link"], 1)
            v.wait_ge(s["spread_link"], 1)
            with v.Fori(0, LOOPS) as t:
                for b in range(2):
                    chunk = 2 * t + b
                    link = Link(v, s["dve_link"], chunk * LINKS)
                    cols = bass.ds(chunk * K, K)
                    nc.vector.tensor_copy(same_c[:], g.same[:, cols])
                    v.wait_ge(s["key_loaded"][b], 16 * (t + 1))
                    v.wait_ge(s["pairs_used"][b], t + 1)
                    nc.vector.tensor_copy(key_f[:, b], key[:, b]).then_inc(s["keys_f"], 1)
                    v.wait_ge(s["keys_f"], chunk + 1)
                    v.wait_ge(s["b_loaded"][b], 16 * (t + 1))
                    for f in range(D):
                        last = nc.vector.tensor_tensor_scan(b_x[:, b, :, f], same_c[:], b_x[:, b, :, f],
                                                            g.seed[:, f:f + 1], ALU.mult, ALU.add)
                    last.then_inc(s["spread_done"][b], 1)
                    v.wait_ge(s["spread_done"][b], t + 1)
                    link(nc.vector.tensor_copy(g.seed[:, 0:D], b_x[:, b, K - 1, :]))
                    for i, (k0, k1) in enumerate(KG):
                        v.wait_ge(s["keys_turned"], len(KG) * chunk + i + 1)
                        pr = nc.vector.tensor_tensor(
                            pairs[:, b, k0:k1, :], ps_key[i % 2][:].rearrange("p (k e) -> p k e", e=P),
                            bc(key_f[:, b, k0:k1], P), ALU.is_equal)
                        pr.then_inc(s["pairs_ready"], 1)
                    v.wait_ge(s["pairs_ready"], len(KG) * (chunk + 1))
                    link(nc.vector.tensor_tensor(earlier[:], pairs[:, b], mid(g.after[:], K), ALU.mult))
                    link(nc.vector.tensor_reduce(again[:], earlier[:], AX.X, ALU.max))
                    link(nc.vector.tensor_scalar(idx_f[:], key_f[:, b], spare[:, 0:1], -1.0, ALU.subtract, ALU.mult))
                    link(nc.vector.tensor_tensor(idx_f[:], idx_f[:], again[:], ALU.mult))
                    link(nc.vector.tensor_tensor(idx_f[:], idx_f[:], key_f[:, b], ALU.add))
                    for r in range(REP):
                        v.wait_ge(added[b][r], 16 * (PER * t + 1))
                    nc.vector.tensor_copy(idx[:, b], idx_f[:]).then_inc(s["idx_ready"][b], 1)
                    assert link.n == LINKS, link.n

        @block.tensor
        def _(pe):
            for b in range(2):
                pe.sem_inc(s["pairs_used"][b], 1)
            with pe.Fori(0, LOOPS) as t:
                for b in range(2):
                    chunk = 2 * t + b
                    pe.wait_ge(s["keys_f"], chunk + 1)
                    for i, (k0, k1) in enumerate(KG):
                        if i >= 2:
                            pe.wait_ge(s["pairs_ready"], len(KG) * chunk + i - 1)
                        for k in range(k0, k1):
                            mm = nc.tensor.matmul(ps_key[i % 2][:, (k - k0) * P:(k - k0 + 1) * P],
                                                  key_f[:, b, k:k + 1].to_broadcast([P, P]), g.ident[:],
                                                  start=True, stop=True)
                        mm.then_inc(s["keys_turned"], 1)
                    pe.wait_ge(s["pairs_ready"], len(KG) * (chunk + 1))
                    pe.wait_ge(s["spread_done"][b], t + 1)
                    pe.wait_ge(s["sums_copied"], chunk + 1)
                    for i, (k0, k1) in enumerate(SG):
                        for k in range(k0, k1):
                            mm = nc.tensor.matmul(ps_sum[:, i, (k - k0) * D:(k - k0 + 1) * D],
                                                  pairs[:, b, k, :], b_x[:, b, k, :], start=True, stop=True)
                    mm.then_inc(s["pairs_used"][b], 1)

        @block.scalar
        def _(act):
            act.sem_inc(s["sums_copied"], 1)
            act.wait_ge(s["zeros_set"], 1)
            act.dma_start(g.d_b96[0:EP, :].rearrange("(p k) w -> p (k w)", p=P).rearrange("p (r x) -> p r x", x=2352),
                          mid(zeros[:], KT * 96 // 2352)).then_inc(s["wide_zeroed"], 16)
            act.dma_start(g.d_b1[0:EP, :].rearrange("(p k) w -> p (k w)", p=P), zeros[:, 0:KT]).then_inc(s["wide_zeroed"], 16)
            with act.Fori(0, LOOPS) as t:
                for b in range(2):
                    act.wait_ge(s["pairs_used"][b], t + 2)
                    for r in range(REP):
                        act.wait_ge(added[b][r], 16 * (PER * t + 1))
                    for i, (k0, k1) in enumerate(SG):
                        cp = nc.scalar.copy(flat(sums[:, b, k0:k1, :]), ps_sum[:, i, 0:(k1 - k0) * D])
                    cp.then_inc(s["sums_copied"], 1)
            act.wait_ge(s["wide_zeroed"], 32)

        @block.gpsimd
        def _(gp):
            for b in range(2):
                for r in range(REP):
                    gp.dma_start(prime[0:1, REP * b + r:REP * b + r + 1], g.d_x[0:1, 0:1]).then_inc(added[b][r], 16)
            with gp.Fori(0, LOOPS) as t:
                for b in range(2):
                    chunk = 2 * t + b
                    gp.wait_ge(s["idx_ready"][b], t + 1)
                    gp.wait_ge(s["sums_copied"], chunk + 2)
                    for k in range(K):
                        r = k % REP
                        if k >= REP:
                            gp.wait_ge(added[b][r], 16 * (PER * t + k // REP + 1))
                        else:
                            gp.wait_ge(added[1 - b][r], 16 * (PER * (t + b) + 1))
                        gp.sem_inc(s["pool_steps"], 1)
                        gp.indirect_dma_start(g.d_acc[r][:, :], offset(idx[:, b, k:k + 1]), sums[:, b, k, :], None,
                                              compute_op=ALU.add).then_inc(added[b][r], 16)
            for r in range(REP):
                for b in range(2):
                    gp.wait_ge(added[b][r], 16 * (PER * LOOPS + 1))


def layer0_nodes(nc, g, a):
    with phase(nc, "loaded dve_link exp_done attended", "sum_loaded") as s:
        relw = s.sbuf("relw", [P, 4, D])
        att_b = s.sbuf("att_b", [P, 1])
        prod = s.sbuf("prod", [P, C, D])
        part = s.sbuf("part", [P, 2, C, D])
        dot = s.sbuf("dot", [P, C])
        att = s.sbuf("att", [P, 2, C])
        rel = s.sbuf("rel", [P, 4])
        block = s.block()
        SUMS = [(ty, r) for ty in range(2) for r in range(REP)]

        @block.sync
        def _(sp):
            sp.dma_start(relw[:], a["rel_rows"].partition_broadcast(P)).then_inc(s["loaded"], 16)
            sp.dma_start(att_b[:], a["att_b"].partition_broadcast(P)).then_inc(s["loaded"], 16)
            for i, (ty, r) in enumerate(SUMS):
                if i >= 2:
                    sp.wait_ge(s["attended"], i - 1)
                sp.dma_start(part[:, i % 2], node_rows(g.d_acc[r][ty * NP:(ty + 1) * NP, :])).then_inc(s["sum_loaded"][i % 2], 16)

        @block.vector
        def _(v):
            link = Link(v, s["dve_link"])
            v.wait_ge(s["loaded"], 32)
            link(nc.vector.tensor_tensor(prod[:], g.x[:], mid(relw[:, 0], C), ALU.mult))
            link(nc.vector.tensor_reduce(dot[:], prod[:], AX.X, ALU.add))
            for ty in range(2):
                link(nc.vector.tensor_tensor(prod[:, 0, :], relw[:, 2 + ty], relw[:, 1], ALU.mult))
                link(nc.vector.tensor_reduce(rel[:, ty:ty + 1], prod[:, 0, :], AX.X, ALU.add))
                link(nc.vector.tensor_tensor(rel[:, ty:ty + 1], rel[:, ty:ty + 1], att_b[:], ALU.add))
                link(nc.vector.tensor_scalar(att[:, ty], dot[:], rel[:, ty:ty + 1], -1.0, ALU.add, ALU.mult))
            link(nc.vector.tensor_copy(rel[:, 2:3], rel[:, 0:1]))
            nc.vector.tensor_copy(rel[:, 3:4], rel[:, 2:3]).then_inc(s["exp_done"], 1)
            v.wait_ge(s["exp_done"], 2)
            link(nc.vector.tensor_scalar(flat(att[:]), flat(att[:]), 1.0, None, ALU.add))
            link(nc.vector.reciprocal(flat(att[:]), flat(att[:])))
            link(nc.vector.memset(g.h[:], 0.0))
            for i, (ty, r) in enumerate(SUMS):
                v.wait_ge(s["sum_loaded"][i % 2], 16 * (i // 2 + 1))
                link(nc.vector.tensor_tensor(prod[:], part[:, i % 2], bc(att[:, ty], D), ALU.mult))
                nc.vector.tensor_tensor(g.h[:], g.h[:], prod[:], ALU.add).then_inc(s["attended"], 1)
                v.wait_ge(s["attended"], i + 1)

        @block.scalar
        def _(act):
            act.wait_ge(s["exp_done"], 1)
            nc.scalar.activation(flat(att[:]), flat(att[:]), ACT.Exp).then_inc(s["exp_done"], 1)


def layernorm(nc, v, link, s, add, out, tmp, stat, gain=None, shift=None):
    link(nc.vector.tensor_tensor(out[:], out[:], add, ALU.add))
    link(nc.vector.tensor_reduce(stat[:, 0], out[:], AX.X, ALU.add))
    link(nc.vector.tensor_scalar(stat[:, 0], stat[:, 0], 1.0 / D, None, ALU.mult))
    nc.vector.tensor_tensor(out[:], out[:], bc(stat[:, 0], D), ALU.subtract).then_inc(s["centred"], 1)
    v.wait_ge(s["squared"], 1)
    link(nc.vector.tensor_reduce(stat[:, 1], tmp[:], AX.X, ALU.add))
    nc.vector.tensor_scalar(stat[:, 1], stat[:, 1], 1.0 / D, 1e-5, ALU.mult, ALU.add).then_inc(s["centred"], 1)
    v.wait_ge(s["squared"], 2)
    link(nc.vector.reciprocal(stat[:, 1], stat[:, 1]))
    last = nc.vector.tensor_tensor(out[:], out[:], bc(stat[:, 1], D), ALU.mult)
    if gain is not None:
        link(last)
        link(nc.vector.tensor_tensor(out[:], out[:], mid(gain, C), ALU.mult))
        last = nc.vector.tensor_tensor(out[:], out[:], mid(shift, C), ALU.add)
    last.then_inc(s["normed"], 1)


def norm_squares(nc, act, s, out, tmp, stat):
    act.wait_ge(s["centred"], 1)
    nc.scalar.activation(flat(tmp[:]), flat(out[:]), ACT.Square).then_inc(s["squared"], 1)
    act.wait_ge(s["centred"], 2)
    nc.scalar.activation(stat[:, 1], stat[:, 1], ACT.Sqrt).then_inc(s["squared"], 1)


def residual(nc, g, add, out, activation=None, gain=None, store=None):
    with phase(nc, "activated dve_link centred squared loaded normed stored") as s:
        tmp = s.sbuf("tmp", [P, C, D])
        stat = s.sbuf("stat", [P, 2, C])
        gs = s.sbuf("gs", [P, 2, D])
        block = s.block()
        @block.sync
        def _(sp):
            if gain is not None:
                sp.dma_start(gs[:], gain.partition_broadcast(P)).then_inc(s["loaded"], 16)
            if store is not None:
                sp.wait_ge(s["normed"], 1)
                sp.dma_start(node_rows(store), out[:]).then_inc(s["stored"], 16)
                sp.wait_ge(s["stored"], 16)

        @block.scalar
        def _(act):
            if activation is not None:
                nc.scalar.activation(flat(add[:]), flat(add[:]), activation).then_inc(s["activated"], 1)
            norm_squares(nc, act, s, out, tmp, stat)

        @block.vector
        def _(v):
            link = Link(v, s["dve_link"])
            if activation is not None:
                v.wait_ge(s["activated"], 1)
            if gain is not None:
                v.wait_ge(s["loaded"], 16)
            layernorm(nc, v, link, s, add[:], out, tmp, stat, *((gs[:, 0], gs[:, 1]) if gain is not None else ()))


def edges(nc, g, kind, a=None, update=False):
    H = NH if kind == "multi" else 1
    FZ = D + H
    R = FZ + H
    table = {"gat": g.d_t66, "dot": g.d_t128, "multi": g.d_t160 if update else g.d_t128}[kind]
    TW = table.shape[1]
    v0 = TW - D if kind != "gat" else 0
    k0 = TW - 2 * D
    spread = {"gat": g.d_b1, "dot": g.d_b64, "multi": g.d_b96 if update else g.d_b64}[kind]
    BW = spread.shape[1]
    states = g.d_e72 if kind == "multi" else g.d_e66
    multi = kind == "multi"
    EW = DE if multi else 1
    G4 = K // 4
    HALVES = ((0, 4), (4, G4))
    turns = 2 if update else 1
    PARTS = 4 if update else 1
    PW = BW // PARTS
    with phase(nc, "pool_steps sp_steps we_read state_init dve_link logits_done exps_done loaded e_turned e_copied "
                   "e_product we_product pre_ready gelu_done centred squared var_ready rooted tail_saved "
                   "b_loaded b_turned spread_done factors_wide states_done states_turned",
               "idx_ready e_loaded gathered rows_used stored e_ready e_stored") as s:
        idx = s.sbuf("idx", [P, 2, K], I32)
        rows = s.sbuf("rows", [P, 2, K, TW])
        b_rows = s.sbuf("b_rows", [P, K, BW])
        b_f = s.sbuf("b_f", [P, 2, BW, K])
        same_w = s.sbuf("same_w", [P, 2, BW, K], BF16)
        values = s.sbuf("values", [P, 2, R, K])
        factors_w = s.sbuf("factors_w", [P, FZ, K])
        state = s.sbuf("state", [P, 2, K, R])
        given = s.sbuf("given", [P, FZ])
        maxima = s.sbuf("maxima", [P, H, K + 1])
        logits = s.sbuf("logits", [P, H, K])
        factors = s.sbuf("factors", [P, 2, H, K])
        prod = s.sbuf("prod", [P, K, D if kind != "gat" else 1])
        e_rows = s.sbuf("e_rows", [P, 2, K, EW])
        e_T = s.sbuf("e_T", [P, G4 if multi else 1, P])
        pre = s.sbuf("pre", [P, K, EW])
        sq = s.sbuf("sq", [P, K, EW])
        stat = s.sbuf("stat", [P, 2, K])
        w_em = s.sbuf("w_em", [P, P if update else 1])
        w_e = s.sbuf("w_e", [P, 16])
        gs = s.sbuf("gs", [P, 2, DE])
        prime = s.sbuf("prime", [1, 4])
        ps_eT = s.psum("ps_eT", [P, 2, 512])
        ps_em = s.psum("ps_em", [P, 2, 512])
        ps_we = s.psum("ps_we", [P, 512])
        block = s.block()

        def e_columns(b, q):
            return e_rows[:, b, 4 * q:4 * q + 4, :].rearrange("p k f -> p (k f)")

        @block.sync
        def _(sp):
            if multi:
                sp.dma_start(w_e[:], a["w_e"]).then_inc(s["loaded"], 16)
                if update:
                    sp.dma_start(w_em[:], a["w_em"]).then_inc(s["loaded"], 16)
                    sp.dma_start(gs[:], a["e_norm"].partition_broadcast(P)).then_inc(s["loaded"], 16)
            for c in range(2):
                if c:
                    sp.wait_ge(s["b_turned"], c)
                sp.dma_start(b_rows[:], edge_rows(spread)[:, c * K:c * K + K, :]).then_inc(s["b_loaded"], 16)
            with sp.Fori(0, LOOPS) as t:
                for b in range(2):
                    chunk = 2 * t + b
                    cols = bass.ds(chunk * K, K)
                    if multi:
                        if update:
                            sp.wait_ge(s["e_stored"][b], 16 * (t + 1))
                        sp.sem_inc(s["sp_steps"], 1)
                        sp.dma_start(e_rows[:, b], edge_rows(g.d_edge)[:, cols, :]).then_inc(s["e_loaded"][b], 16)
                    sp.wait_ge(s["b_turned"], chunk + 2)
                    sp.dma_start(b_rows[:], edge_rows_after(spread, 2 * K)[:, cols, :]).then_inc(s["b_loaded"], 16)
            if update:
                sp.wait_ge(s["e_stored"][0], 16 * (LOOPS + 1))
                sp.dma_start(e_rows[:, 0], edge_rows(g.d_edge)[:, 0:K, :]).then_inc(s["e_loaded"][0], 16)

        @block.gpsimd
        def _(gp):
            with gp.Fori(0, LOOPS) as t:
                for b in range(2):
                    gp.wait_ge(s["rows_used"][b], t + 1)
                    gp.wait_ge(s["idx_ready"][b], t + 1)
                    gp.sem_inc(s["pool_steps"], 1)
                    for k in range(K):
                        gp.indirect_dma_start(rows[:, b, k, :], None, table[:, :],
                                              offset(idx[:, b, k:k + 1])).then_inc(s["gathered"][b], 16)

        @block.scalar
        def _(act):
            def turn_e(n):
                for half, (q0, q1) in enumerate(HALVES):
                    act.wait_ge(s["e_turned"], 2 * n + half + 1)
                    nc.scalar.copy(flat(e_T[:, q0:q1, :]), ps_eT[:, half, 0:(q1 - q0) * P]).then_inc(s["e_copied"], 1)

            def turn_b(chunk, b, start):
                nc.scalar.copy(same_w[:, b, :, 1:], g.same[:, bass.ds(start + 1, K - 1)].unsqueeze(1)
                               .to_broadcast([P, BW, K - 1]))
                act.wait_ge(s["b_loaded"], 16 * (chunk + 1))
                nc.scalar.copy(b_f[:, b], b_rows[:].rearrange("p k f -> p f k")).then_inc(s["b_turned"], 1)

            for b in range(2):
                act.dma_start(prime[0:1, b:b + 1], g.d_x[0:1, 0:1]).then_inc(s["stored"][b], 16)
                if update:
                    act.dma_start(prime[0:1, 2 + b:3 + b], g.d_x[0:1, 0:1]).then_inc(s["e_stored"][b], 16)
            act.wait_ge(s["state_init"], 1)
            turn_b(0, 0, 0)
            turn_b(1, 1, K)
            if update:
                turn_e(0)
            with act.Fori(0, LOOPS) as t:
                for b in range(2):
                    chunk = 2 * t + b
                    cols = bass.ds(chunk * K, K)
                    if multi and not update:
                        turn_e(chunk)
                    if update:
                        act.wait_ge(s["pre_ready"], chunk + 1)
                        nc.scalar.activation(flat(pre[:]), flat(pre[:]), ACT.Gelu_apprx_tanh).then_inc(s["gelu_done"], 1)
                        act.wait_ge(s["centred"], chunk + 1)
                        nc.scalar.activation(flat(sq[:]), flat(pre[:]), ACT.Square).then_inc(s["squared"], 1)
                        act.wait_ge(s["var_ready"], chunk + 1)
                        nc.scalar.activation(stat[:, 1], stat[:, 1], ACT.Sqrt).then_inc(s["rooted"], 1)
                        turn_e(2 * chunk + 1)
                        act.wait_ge(s["e_ready"][b], t + 1)
                        act.dma_start(edge_rows(g.d_edge)[:, cols, :], e_rows[:, b]).then_inc(s["e_stored"][b], 16)
                    act.wait_ge(s["logits_done"], chunk + 1)
                    f = factors[:].rearrange("p a h k -> p (a h k)")
                    nc.scalar.activation(f, f, ACT.Exp).then_inc(s["exps_done"], 1)
                    act.wait_ge(s["exps_done"], chunk + 1)
                    for h in range(H):
                        nc.scalar.copy(factors_w[:, h * D // H:(h + 1) * D // H, 1:],
                                       mid(factors[:, 0, h, 1:], D // H))
                    nc.scalar.copy(factors_w[:, D:FZ, 1:], factors[:, 0, :, 1:]).then_inc(s["factors_wide"], 1)
                    if update:
                        turn_e(2 * chunk + 2)
                    act.wait_ge(s["spread_done"], (PARTS + 1) * (chunk + 1) + 1)
                    turn_b(chunk + 2, b, (chunk + 2) * K)
                    act.wait_ge(s["stored"][b], 16 * (t + 1))
                    act.wait_ge(s["states_done"], chunk + 1)
                    nc.scalar.copy(state[:, b], values[:, b].rearrange("p f k -> p k f")).then_inc(s["states_turned"], 1)
                    act.wait_ge(s["states_turned"], chunk + 3)
                    act.dma_start(edge_rows(states)[:, cols, :], state[:, b]).then_inc(s["stored"][b], 16)
            for b in range(2):
                act.wait_ge(s["stored"][b], 16 * (LOOPS + 1))
                if update:
                    act.wait_ge(s["e_stored"][b], 16 * (LOOPS + 1))

        @block.tensor
        def _(pe):
            if not multi:
                return
            pe.wait_ge(s["loaded"], 16 * (3 if update else 1))

            def turn(n, b):
                for half, (q0, q1) in enumerate(HALVES):
                    for q in range(q0, q1):
                        mm = nc.tensor.transpose(ps_eT[:, half, (q - q0) * P:(q - q0 + 1) * P],
                                                 e_columns(b, q), g.ident[:])
                    mm.then_inc(s["e_turned"], 1)
                pe.wait_ge(s["e_copied"], 2 * (n + 1))

            def old_product(chunk, b, round_, again=True):
                pe.wait_ge(s["e_loaded"][b], 16 * (round_ + 1))
                turn(2 * chunk, b)
                if again:
                    pe.wait_ge(s["pre_ready"], chunk)
                for q in range(G4):
                    mm = nc.tensor.matmul(ps_em[:, q // 4, (q % 4) * P:(q % 4 + 1) * P], e_T[:, q, :],
                                          w_em[:], start=True, stop=True)
                mm.then_inc(s["e_product"], 1)

            if update:
                old_product(0, 0, 0, False)
            with pe.Fori(0, LOOPS) as t:
                for b in range(2):
                    chunk = 2 * t + b
                    if update:
                        pe.wait_ge(s["e_product"], chunk + 1)
                        pe.wait_ge(s["e_ready"][b], t + 1)
                        turn(2 * chunk + 1, b)
                    else:
                        pe.wait_ge(s["e_loaded"][b], 16 * (t + 1))
                        turn(chunk, b)
                    pe.wait_ge(s["we_read"], chunk + 1)
                    for q in range(G4):
                        mm = nc.tensor.matmul(ps_we[:, q * 16:(q + 1) * 16], e_T[:, q, :], w_e[:],
                                              start=True, stop=True)
                    mm.then_inc(s["we_product"], 1)
                    if update:
                        old_product(chunk + 1, 1 - b, t + b)

        LINKS = {"gat": 6, "dot": 7, "multi": 14 if update else 6}[kind]

        @block.vector
        def _(v):
            nc.vector.memset(maxima[:], -BIG)
            nc.vector.memset(values[:, 1], 0.0)
            nc.vector.memset(factors_w[:, :, 0:1], 0.0)
            nc.vector.memset(same_w[:, :, :, 0:1], 0.0).then_inc(s["state_init"], 1)
            for b in range(2):
                v.sem_inc(s["rows_used"][b], 1)
                v.sem_inc(s["states_turned"], 1)
            v.sem_inc(s["we_read"], 1)
            for b in range(2):
                nc.vector.tensor_copy(idx[:, b], g.src[:, b * K:b * K + K]).then_inc(s["idx_ready"][b], 1)
            v.wait_ge(s["state_init"], 1)
            if update:
                v.wait_ge(s["loaded"], 48)

            def spread_part(chunk, b, start, i, before):
                if i == 0:
                    v.wait_ge(s["b_turned"], chunk + 1)
                    first = b_f[:, b, :, 0]
                    nc.vector.scalar_tensor_tensor(first, before, g.same[:, bass.ds(start, 1)], first,
                                                   ALU.mult, ALU.add).then_inc(s["spread_done"], 1)
                    v.wait_ge(s["spread_done"], (PARTS + 1) * chunk + 1)
                part = b_f[:, b, i * PW:(i + 1) * PW, :].rearrange("p f k -> p (f k)")
                mask = same_w[:, b, i * PW:(i + 1) * PW, :].rearrange("p f k -> p (f k)")
                nc.vector.tensor_tensor_scan(part, mask, part, 0.0, ALU.mult, ALU.add).then_inc(s["spread_done"], 1)

            for i in range(PARTS):
                spread_part(0, 0, 0, i, g.seed[:, 0:BW])
            with v.Fori(0, LOOPS) as t:
                for b in range(2):
                    chunk = 2 * t + b
                    link = Link(v, s["dve_link"], chunk * LINKS)
                    G, B, V = rows[:, b], b_f[:, b].rearrange("p f k -> p k f"), values[:, b]
                    cut_c = g.cut[:, bass.ds(chunk * K, K)]

                    def spread_next(i):
                        spread_part(chunk + 1, 1 - b, (chunk + 1) * K, i, b_f[:, b, :, K - 1])

                    v.wait_ge(s["spread_done"], (PARTS + 1) * (chunk + 1))
                    v.wait_ge(s["gathered"][b], 16 * K * (t + 1))
                    nc.vector.tensor_copy(idx[:, b], g.src[:, bass.ds((chunk + 2) * K, K)]).then_inc(s["idx_ready"][b], 1)
                    if update:
                        e = e_rows[:, b]
                        link(nc.vector.tensor_tensor(pre[:], G[:, :, 0:DE], B[:, :, D:D + DE], ALU.add))
                        v.wait_ge(s["e_product"], chunk + 1)
                        nc.vector.tensor_tensor(flat(pre[:]), flat(pre[:]),
                                                ps_em[:].rearrange("p a x -> p (a x)")[:, 0:K * DE],
                                                ALU.add).then_inc(s["pre_ready"], 1)
                        spread_next(0)
                        spread_next(1)
                        v.wait_ge(s["gelu_done"], chunk + 1)
                        link(nc.vector.tensor_tensor(pre[:], pre[:], e, ALU.add))
                        link(nc.vector.tensor_reduce(stat[:, 0], pre[:], AX.X, ALU.add))
                        link(nc.vector.tensor_scalar(stat[:, 0], stat[:, 0], 1.0 / DE, None, ALU.mult))
                        nc.vector.tensor_tensor(pre[:], pre[:], bc(stat[:, 0], DE), ALU.subtract).then_inc(s["centred"], 1)
                        spread_next(2)
                        v.wait_ge(s["squared"], chunk + 1)
                        link(nc.vector.tensor_reduce(stat[:, 1], sq[:], AX.X, ALU.add))
                        nc.vector.tensor_scalar(stat[:, 1], stat[:, 1], 1.0 / DE, 1e-5, ALU.mult, ALU.add).then_inc(s["var_ready"], 1)
                        v.wait_ge(s["centred"], chunk + 1)
                        link(nc.vector.tensor_tensor(pre[:], pre[:], mid(gs[:, 0], K), ALU.mult))
                        v.wait_ge(s["rooted"], chunk + 1)
                        link(nc.vector.reciprocal(stat[:, 1], stat[:, 1]))
                        link(nc.vector.tensor_tensor(pre[:], pre[:], bc(stat[:, 1], DE), ALU.mult))
                        nc.vector.tensor_tensor(e, pre[:], mid(gs[:, 1], K), ALU.add).then_inc(s["e_ready"][b], 1)
                    if kind == "gat":
                        link(nc.vector.tensor_tensor(logits[:, 0], G[:, :, D], B[:, :, 0], ALU.add))
                        spread_next(0)
                        link(nc.vector.scalar_tensor_tensor(logits[:, 0], logits[:, 0], 0.2, logits[:, 0], ALU.mult, ALU.max))
                    else:
                        link(nc.vector.tensor_tensor(prod[:], G[:, :, k0:k0 + D], B[:, :, 0:D], ALU.mult))
                        link(nc.vector.tensor_reduce(logits[:].rearrange("p h k -> p k h"),
                                                     prod[:].rearrange("p k (h d) -> p k h d", h=H), AX.X, ALU.add))
                        if kind == "dot":
                            link(nc.vector.scalar_tensor_tensor(logits[:, 0], logits[:, 0], 0.2, logits[:, 0],
                                                                ALU.mult, ALU.max))
                    if multi:
                        v.wait_ge(s["we_product"], chunk + 1)
                        nc.vector.scalar_tensor_tensor(
                            logits[:], logits[:], 0.25, ps_we[:, 0:K * NH].rearrange("p (k h) -> p h k", h=NH),
                            ALU.mult, ALU.add).then_inc(s["we_read"], 1)
                        v.wait_ge(s["we_read"], chunk + 2)
                    for h in range(H):
                        last = nc.vector.tensor_tensor_scan(maxima[:, h, 1:], cut_c, logits[:, h], maxima[:, h, 0:1],
                                                            ALU.add, ALU.max)
                    link(last)
                    nc.vector.tensor_tensor(factors[:, 1], logits[:], maxima[:, :, 1:], ALU.subtract)
                    link(nc.vector.tensor_tensor(factors[:, 0], maxima[:, :, 0:K], mid(cut_c, H), ALU.add))
                    nc.vector.tensor_tensor(factors[:, 0], factors[:, 0], maxima[:, :, 1:], ALU.subtract).then_inc(s["logits_done"], 1)
                    if kind != "gat":
                        spread_next(PARTS - 1)
                    v.wait_ge(s["logits_done"], chunk + 1)
                    v.wait_ge(s["states_turned"], chunk + 1)
                    nc.vector.tensor_copy(V[:, FZ:R, :], maxima[:, :, 1:])
                    nc.vector.tensor_copy(maxima[:, :, 0:1], maxima[:, :, K:K + 1])
                    v.wait_ge(s["exps_done"], chunk + 1)
                    weights = factors[:, 1].unsqueeze(2).to_broadcast([P, H, D // H, K])
                    nc.vector.tensor_copy(V[:, D:FZ, :], factors[:, 1])
                    nc.vector.tensor_tensor(V[:, 0:D, :].rearrange("p (h d) k -> p h d k", h=H),
                                            G[:, :, v0:v0 + D].rearrange("p k (h d) -> p h d k", h=H),
                                            weights, ALU.mult).then_inc(s["rows_used"][b], 1)
                    before = values[:, 1 - b, 0:FZ, K - 1]
                    nc.vector.tensor_tensor(given[:, 0:D].rearrange("p (h d) -> p h d", h=H),
                                            before[:, 0:D].rearrange("p (h d) -> p h d", h=H),
                                            bc(factors[:, 0, :, 0], D // H), ALU.mult)
                    link(nc.vector.tensor_tensor(given[:, D:FZ], before[:, D:FZ], factors[:, 0, :, 0], ALU.mult))
                    v.wait_ge(s["rows_used"][b], t + 2)
                    link(nc.vector.tensor_tensor(V[:, 0:FZ, 0], V[:, 0:FZ, 0], given[:], ALU.add))
                    v.wait_ge(s["factors_wide"], chunk + 1)
                    nc.vector.tensor_tensor_scan(V[:, 0:FZ, :].rearrange("p f k -> p (f k)"), flat(factors_w[:]),
                                                 V[:, 0:FZ, :].rearrange("p f k -> p (f k)"), 0.0,
                                                 ALU.mult, ALU.add).then_inc(s["states_done"], 1)
                    v.wait_ge(s["states_done"], chunk + 1)
                    assert link.n == LINKS, (kind, update, link.n)
            nc.vector.tensor_copy(g.tail[:, 0:R], values[:, 1, :, K - 1]).then_inc(s["tail_saved"], 1)
            v.wait_ge(s["tail_saved"], 1)


def join(nc, g, H, states):
    FZ = D + H
    R = FZ + H
    with phase(nc, "dve_link turned scanned exp_done back_turned boundary written collected") as s:
        wide = s.sbuf("wide", [P, FZ])
        mx = s.sbuf("mx", [FZ, P + 1])
        sm = s.sbuf("sm", [FZ, P + 1])
        fac = s.sbuf("fac", [FZ, 2, P])
        edge_state = s.sbuf("edge_state", [P, R])
        given = s.sbuf("given", [P, 2, FZ])
        fac2 = s.sbuf("fac2", [P, 2, FZ])
        both = s.sbuf("both", [P, FZ])
        merged = s.sbuf("merged", [P, R])
        ps_t = s.psum("ps_t", [P, 512])
        ps_b = s.psum("ps_b", [P, 512])
        block = s.block()
        def widen(v, link, src, out):
            nc.vector.tensor_copy(out[:, 0:D].rearrange("p (h d) -> p h d", h=H), bc(src, D // H))
            link(nc.vector.tensor_copy(out[:, D:FZ], src))

        @block.vector
        def _(v):
            link = Link(v, s["dve_link"])
            widen(v, link, g.tail[:, FZ:R], wide)
            nc.vector.memset(mx[:, 0:1], -BIG)
            link(nc.vector.memset(sm[:, 0:1], 0.0))
            v.wait_ge(s["turned"], 1)
            link(nc.vector.tensor_tensor_scan(mx[:, 1:], g.pass_cut[0:FZ, :], ps_t[0:FZ, P:2 * P], mx[:, 0:1],
                                              ALU.add, ALU.max))
            nc.vector.tensor_tensor(fac[:, 1], ps_t[0:FZ, P:2 * P], mx[:, 1:], ALU.subtract)
            link(nc.vector.tensor_tensor(fac[:, 0], mx[:, 0:P], g.pass_cut[0:FZ, :], ALU.add))
            nc.vector.tensor_tensor(fac[:, 0], fac[:, 0], mx[:, 1:], ALU.subtract).then_inc(s["scanned"], 1)
            v.wait_ge(s["exp_done"], 1)
            link(nc.vector.tensor_tensor(fac[:, 1], fac[:, 1], ps_t[0:FZ, 0:P], ALU.mult))
            nc.vector.tensor_tensor_scan(sm[:, 1:], fac[:, 0], fac[:, 1], sm[:, 0:1], ALU.mult, ALU.add).then_inc(s["scanned"], 1)
            v.wait_ge(s["back_turned"], 1)
            link(nc.vector.tensor_copy(flat(given[:]), ps_b[:, 0:2 * FZ]))
            v.wait_ge(s["boundary"], 16)
            widen(v, link, edge_state[:, FZ:R], wide)
            link(nc.vector.tensor_tensor(both[:], wide[:], given[:, 1], ALU.max))
            nc.vector.tensor_tensor(fac2[:, 0], wide[:], both[:], ALU.subtract)
            nc.vector.tensor_tensor(fac2[:, 1], given[:, 1], both[:], ALU.subtract).then_inc(s["scanned"], 1)
            v.wait_ge(s["exp_done"], 2)
            nc.vector.tensor_tensor(fac2[:, 0], fac2[:, 0], edge_state[:, 0:FZ], ALU.mult)
            link(nc.vector.tensor_tensor(fac2[:, 1], fac2[:, 1], given[:, 0], ALU.mult))
            nc.vector.tensor_tensor(merged[:, 0:FZ], fac2[:, 0], fac2[:, 1], ALU.add)
            nc.vector.tensor_copy(merged[:, FZ:R], both[:, D:FZ]).then_inc(s["scanned"], 1)

        @block.scalar
        def _(act):
            act.wait_ge(s["scanned"], 1)
            nc.scalar.activation(flat(fac[:]), flat(fac[:]), ACT.Exp).then_inc(s["exp_done"], 1)
            act.wait_ge(s["scanned"], 3)
            nc.scalar.activation(flat(fac2[:]), flat(fac2[:]), ACT.Exp).then_inc(s["exp_done"], 1)

        @block.tensor
        def _(pe):
            pe.wait_ge(s["dve_link"], 1)
            nc.tensor.transpose(ps_t[0:FZ, 0:P], g.tail[:, 0:FZ], g.ident[:])
            nc.tensor.transpose(ps_t[0:FZ, P:2 * P], wide[:], g.ident[:]).then_inc(s["turned"], 1)
            pe.wait_ge(s["scanned"], 2)
            nc.tensor.transpose(ps_b[:, 0:FZ], sm[:, 0:P], g.ident[0:FZ, 0:FZ])
            nc.tensor.transpose(ps_b[:, FZ:2 * FZ], mx[:, 0:P], g.ident[0:FZ, 0:FZ]).then_inc(s["back_turned"], 1)

        @block.gpsimd
        def _(gp):
            gp.indirect_dma_start(edge_state[:], None, states[:, :], offset(g.idx_join[:])).then_inc(s["boundary"], 16)
            gp.wait_ge(s["boundary"], 16)
            gp.wait_ge(s["scanned"], 4)
            gp.indirect_dma_start(states[:, :], offset(g.idx_join[:]), merged[:], None).then_inc(s["written"], 16)
            gp.wait_ge(s["written"], 16)
            for c in range(C):
                gp.indirect_dma_start(g.node_state(R)[:, c, :], None, states[:, :],
                                      offset(g.idx_last[:, c:c + 1])).then_inc(s["collected"], 16)
            gp.wait_ge(s["collected"], 16 * C)


def gat_nodes(nc, g, bias, gelu):
    st = g.node_state(66)
    with phase(nc, "loaded dve_link shifted exp_done summed gelu_done") as s:
        bias_sb = s.sbuf("bias", [P, D])
        ls = s.sbuf("ls", [P, 3, C])
        fac = s.sbuf("fac", [P, 2, C])
        own = s.sbuf("own", [P, C, D])
        block = s.block()
        @block.sync
        def _(sp):
            sp.dma_start(bias_sb[:], bias.partition_broadcast(P)).then_inc(s["loaded"], 16)

        @block.vector
        def _(v):
            link = Link(v, s["dve_link"])
            h, m, z = g.proj, st[:, :, 65], st[:, :, 64]
            link(nc.vector.tensor_tensor(ls[:, 0], h[:, :, 64], h[:, :, 65], ALU.add))
            link(nc.vector.scalar_tensor_tensor(ls[:, 0], ls[:, 0], 0.2, ls[:, 0], ALU.mult, ALU.max))
            link(nc.vector.tensor_tensor(ls[:, 1], ls[:, 0], m, ALU.max))
            nc.vector.tensor_tensor(fac[:, 0], m, ls[:, 1], ALU.subtract)
            nc.vector.tensor_tensor(fac[:, 1], ls[:, 0], ls[:, 1], ALU.subtract).then_inc(s["shifted"], 1)
            v.wait_ge(s["exp_done"], 1)
            link(nc.vector.tensor_tensor(ls[:, 2], z, fac[:, 0], ALU.mult))
            link(nc.vector.tensor_tensor(ls[:, 2], ls[:, 2], fac[:, 1], ALU.add))
            link(nc.vector.reciprocal(ls[:, 2], ls[:, 2]))
            link(nc.vector.tensor_tensor(fac[:], fac[:], mid(ls[:, 2], 2), ALU.mult))
            nc.vector.tensor_tensor(own[:], h[:, :, 0:D], bc(fac[:, 1], D), ALU.mult)
            link(nc.vector.tensor_tensor(st[:, :, 0:D], st[:, :, 0:D], bc(fac[:, 0], D), ALU.mult))
            link(nc.vector.tensor_tensor(own[:], own[:], st[:, :, 0:D], ALU.add))
            v.wait_ge(s["loaded"], 16)
            nc.vector.tensor_tensor(g.h[:], own[:], mid(bias_sb[:], C), ALU.add).then_inc(s["summed"], 1)

        @block.scalar
        def _(act):
            act.wait_ge(s["shifted"], 1)
            nc.scalar.activation(flat(fac[:]), flat(fac[:]), ACT.Exp).then_inc(s["exp_done"], 1)
            if gelu:
                act.wait_ge(s["summed"], 1)
                nc.scalar.activation(flat(g.h[:]), flat(g.h[:]), ACT.Gelu).then_inc(s["gelu_done"], 1)


def divide(nc, g, H, out):
    st = g.node_state(D + 2 * H)
    with phase(nc, "dve_link") as s:
        rec = s.sbuf("rec", [P, C, H])
        block = s.block()
        @block.vector
        def _(v):
            link = Link(v, s["dve_link"])
            link(nc.vector.tensor_scalar(rec[:], st[:, :, D:D + H], 1e-9, None, ALU.add))
            link(nc.vector.reciprocal(rec[:], rec[:]))
            for h in range(H):
                w = D // H
                last = nc.vector.tensor_tensor(out[:, :, h * w:(h + 1) * w], st[:, :, h * w:(h + 1) * w],
                                               bc(rec[:, :, h], w), ALU.mult)
            link(last)


def stack_features(nc, g, out):
    with phase(nc, "stacked") as s:
        block = s.block()
        @block.vector
        def _(v):
            nc.vector.tensor_copy(out[:, :, 0:D], g.x[:])
            nc.vector.tensor_copy(out[:, :, D:2 * D], g.h[:]).then_inc(s["stacked"], 1)
            v.wait_ge(s["stacked"], 1)


def copy_nodes(nc, src, dst):
    with phase(nc, "copied") as s:
        block = s.block()
        @block.vector
        def _(v):
            nc.vector.tensor_copy(dst[:], src[:]).then_inc(s["copied"], 1)
            v.wait_ge(s["copied"], 1)


class Graph:

    def node_state(self, width):
        return self.states_sb[:, :, 0:width]


def build(nc, a, out):
    g = Graph()
    with ExitStack() as ctx:
        def sb(name, shape, dt=F32):
            return ctx.enter_context(nc.sbuf_tensor(name, shape, dt))

        def dram(name, shape, dt=F32):
            return nc.dram_tensor(name, shape, dt, kind="Internal").ap()

        g.x, g.h = sb("x", [P, C, D]), sb("h", [P, C, D])
        g.states_sb = sb("states_sb", [P, C, 72])
        g.ident, g.ones, g.iota = sb("ident", [P, P]), sb("ones", [P, P]), sb("iota", [P, P])
        g.before, g.after = sb("before", [P, P]), sb("after", [P, P])
        g.pcol = sb("pcol", [P, 1])
        g.same, g.cut = sb("same", [P, KT + 2 * K]), sb("cut", [P, KT])
        g.src = sb("src", [P, KT + 2 * K], I32)
        g.pass_cut = sb("pass_cut", [68, P])
        g.dst0, g.idx_join = sb("dst0", [P, 1], I32), sb("idx_join", [P, 1], I32)
        g.idx_first, g.idx_last = sb("idx_first", [P, C], I32), sb("idx_last", [P, C], I32)
        g.seed, g.tail = sb("seed", [P, 96]), sb("tail", [P, 72])
        g.gat_w = sb("gat_w", [P, 2, D + 2])
        g.d_key = dram("d_key", [P, KT], I32)
        g.d_src, g.d_x = a["src_pad"], a["x_pad"]
        g.d_acc = [dram(f"d_acc{r}", [ACC_ROWS, D]) for r in range(REP)]
        g.d_b1, g.d_b64, g.d_b96 = (dram(f"d_b{w}", [B_ROWS, w]) for w in (1, 64, 96))
        g.d_e66, g.d_e72 = (dram(f"d_e{w}", [E_ROWS, w]) for w in (66, 72))
        g.d_t66, g.d_t128, g.d_t160 = (dram(f"d_t{w}", [NP, w]) for w in (66, 128, 160))
        g.d_q64, g.d_q96 = dram("d_q64", [NP, 64]), dram("d_q96", [NP, 96])
        g.d_edge = dram("d_edge", [EP, DE])


        prepare(nc, g, a)
        spread_x(nc, g)
        layer0_edges(nc, g)
        layer0_nodes(nc, g, a)
        with scratch(nc, "l0_out", [P, C, D]) as l0_out:
            project(nc, g, g.h, D, a["l0_w"], True, D, l0_out)
            residual(nc, g, l0_out, g.x, activation=ACT.Tanh)

        copy_nodes(nc, g.x, g.h)
        with scratch(nc, "proj", [P, C, D + 2]) as proj:
            g.proj = proj
            gat = dict(table=(g.d_t66, 0, D + 2), spread=(g.d_b1, D + 1, D + 2))
            with scratch(nc, "seed66", [P, D + 2]) as seed66:
                def gat_project(rows, width, w):
                    project(nc, g, rows, width, w, False, D + 2, proj, seed=(g.d_t66, None, seed66[:]), from_sbuf=True, **gat)
                    with phase(nc, "seed_set") as s:
                        block = s.block()
                        @block.vector
                        def _(v):
                            nc.vector.tensor_copy(g.seed[:, 0:1], seed66[:, D + 1:D + 2]).then_inc(s["seed_set"], 1)
                            v.wait_ge(s["seed_set"], 1)

                def gat_edges():
                    edges(nc, g, "gat")
                    join(nc, g, 1, g.d_e66)

                with nc.Fori(0, 4):
                    gat_project(g.h, D, g.gat_w[0:D, 1, :])
                    gat_edges()
                    gat_nodes(nc, g, a["b_std"], True)
                with scratch(nc, "stacked", [P, C, 2 * D]) as stacked:
                    stack_features(nc, g, stacked)
                    gat_project(stacked, 2 * D, g.gat_w[:, 0, :])
                gat_edges()
            gat_nodes(nc, g, a["b_skip"], False)
        residual(nc, g, g.h, g.x)

        with scratch(nc, "proj", [P, C, 3 * D]) as proj:
            project(nc, g, g.x, D, a["l2_w"], True, 3 * D, proj, table=(g.d_t128, 0, 2 * D),
                    spread=(g.d_b64, 2 * D, 3 * D), seed=(g.d_q64, (2 * D, 3 * D), g.seed[:, 0:D]))
        edges(nc, g, "dot")
        join(nc, g, 1, g.d_e66)
        divide(nc, g, 1, g.h)
        residual(nc, g, g.h, g.x)

        copy_nodes(nc, g.x, g.h)
        with phase(nc, "copied") as s:
            block = s.block()
            @block.sync
            def _(sp):
                sp.dma_start(g.d_edge[:, :], a["edge_pad"]).then_inc(s["copied"], 16)
                sp.wait_ge(s["copied"], 16)

        def multi_layer(i, update):
            w = {k: a[k][i] for k in ("w_e", "w_em", "e_norm", "w_o", "h_norm")}
            if update:
                with scratch(nc, "proj", [P, C, 256]) as proj:
                    project(nc, g, g.h, D, a["l3_w"][i], True, 256, proj, table=(g.d_t160, 0, 160),
                            spread=(g.d_b96, 160, 256), seed=(g.d_q96, (160, 256), g.seed[:, 0:96]))
            else:
                with scratch(nc, "proj", [P, C, 192]) as proj:
                    project(nc, g, g.h, D, a["l3_w0"], True, 192, proj, table=(g.d_t128, 0, 128),
                            spread=(g.d_b64, 128, 192), seed=(g.d_q64, (128, 192), g.seed[:, 0:D]))
            edges(nc, g, "multi", w, update)
            join(nc, g, NH, g.d_e72)
            with scratch(nc, "agg", [P, C, D]) as agg:
                divide(nc, g, NH, agg)
                with scratch(nc, "delta", [P, C, D]) as delta:
                    project(nc, g, agg, D, w["w_o"], False, D, delta)
                    residual(nc, g, delta, g.h, gain=w["h_norm"])

        multi_layer(0, False)
        with nc.Fori(1, 3) as i:
            multi_layer(i, True)
        residual(nc, g, g.h, g.x, store=out)


_OUT = ((N, D), "float32")


def lay_out(x, src, dst, edge_attr_32, edge_type_2, L0_gnn_relation_emb, L0_gnn_att_w, L0_gnn_att_b, L0_gnn_W_w,
            L0_gnn_W_b, L1_gnn_W_std, L1_gnn_a_src_std, L1_gnn_a_dst_std, L1_gnn_b_std, L1_gnn_W_skip,
            L1_gnn_a_src_skip, L1_gnn_a_dst_skip, L1_gnn_b_skip, L2_gnn_Wq, L2_gnn_bq, L2_gnn_Wk, L2_gnn_bk,
            L2_gnn_Wf, L2_gnn_bf, L3_gnn_Wq, L3_gnn_Wk, L3_gnn_Wv, L3_gnn_Wo, L3_gnn_We, L3_gnn_Wem, L3_gnn_bem,
            L3_gnn_gn, L3_gnn_bn, L3_gnn_ge, L3_gnn_be):
    def padded(v, shape, fill=0):
        out = np.full(shape, fill, v.dtype)
        out[tuple(slice(0, n) for n in v.shape)] = v
        return out

    ids = np.full(EP + 2, NP - 1, np.int32)
    ids[0] = -1
    ids[1:E + 1] = dst
    f = np.float32
    L = L3_gnn_Wq.shape[0]
    l3_w = np.zeros((L, D + 1, 256), f)
    w_em = np.zeros((L, P, P), f)
    e_norm = np.zeros((L, 2, DE), f)
    w_e = np.zeros((L, P, 16), f)
    for i in range(L):
        l3_w[i, 0:D, 32:96], l3_w[i, 0:D, 96:160], l3_w[i, 0:D, 160:224] = L3_gnn_Wk[i], L3_gnn_Wv[i], L3_gnn_Wq[i]
        for q in range(4):
            w_e[i, 32 * q:32 * q + 32, 4 * q:4 * q + 4] = L3_gnn_We[i]
        if i:
            l3_w[i, 0:D, 0:32], l3_w[i, 0:D, 224:256] = L3_gnn_Wem[i - 1, 0:D], L3_gnn_Wem[i - 1, D:2 * D]
            l3_w[i, D, 224:256] = L3_gnn_bem[i - 1]
            e_norm[i, 0], e_norm[i, 1] = L3_gnn_ge[i - 1], L3_gnn_be[i - 1]
            for q in range(4):
                w_em[i, 32 * q:32 * q + 32, 32 * q:32 * q + 32] = L3_gnn_Wem[i - 1, 2 * D:]
    l3_w0 = np.zeros((D + 1, 192), f)
    l3_w0[0:D] = l3_w[0, 0:D, 32:224]
    l2_w = np.zeros((D + 1, 192), f)
    for j, (w, b) in enumerate(((L2_gnn_Wk, L2_gnn_bk), (L2_gnn_Wf, L2_gnn_bf), (L2_gnn_Wq, L2_gnn_bq))):
        l2_w[0:D, 64 * j:64 * j + 64], l2_w[D, 64 * j:64 * j + 64] = w, b
    return {
        "x_pad": padded(x, (NP, D)),
        "dst_ext": np.stack([ids[p * KT:p * KT + KT + 2] for p in range(P)]),
        "src_pad": padded(src, (EP,), NP - 1).reshape(P, KT),
        "type_pad": padded(edge_type_2, (EP,)).reshape(P, KT),
        "edge_pad": padded(edge_attr_32, (EP, DE)),
        "rel_rows": np.concatenate([L0_gnn_att_w.reshape(2, D), L0_gnn_relation_emb]),
        "att_b": L0_gnn_att_b,
        "l0_w": np.concatenate([L0_gnn_W_w.T, L0_gnn_W_b[None]]),
        "gat_w_skip": L1_gnn_W_skip, "gat_w_std": L1_gnn_W_std,
        "gat_wT": np.concatenate([L1_gnn_W_skip.T, L1_gnn_W_std.T], 1),
        "gat_a": np.stack([L1_gnn_a_src_skip, L1_gnn_a_dst_skip, L1_gnn_a_src_std, L1_gnn_a_dst_std], 1),
        "b_std": L1_gnn_b_std, "b_skip": L1_gnn_b_skip,
        "l2_w": l2_w, "l3_w0": l3_w0, "l3_w": l3_w, "w_e": w_e, "w_em": w_em, "e_norm": e_norm,
        "w_o": L3_gnn_Wo, "h_norm": np.stack([L3_gnn_gn, L3_gnn_bn], 1),
    }


def kernel(**inputs):
    import concourse.bacc as bacc
    from concourse.bass_utils import run_bass_kernel_spmd

    laid = {k: np.ascontiguousarray(v) for k, v in lay_out(**{k: np.asarray(v) for k, v in inputs.items()}).items()}
    nc = bacc.Bacc("TRN2", target_bir_lowering=False, num_devices=1)
    aps = {k: nc.dram_tensor(f"in_{k}", v.shape, mybir.dt.from_np(v.dtype), kind="ExternalInput").ap()
           for k, v in laid.items()}
    out = nc.dram_tensor("out_0", (NP, D), F32, kind="ExternalOutput").ap()
    build(nc, aps, out)
    r = run_bass_kernel_spmd(nc, [{f"in_{k}": v for k, v in laid.items()}], core_ids=[0])
    return np.ascontiguousarray(r.results[0]["out_0"][0:N])
```

```python
from contextlib import ExitStack, contextmanager

import numpy as np
import concourse.bass as bass
from concourse import mybir

F32 = mybir.dt.float32
I32 = mybir.dt.int32
BF16 = mybir.dt.bfloat16
ALU = mybir.AluOpType
ACT = mybir.ActivationFunctionType
AX = mybir.AxisListType

P = 128
N, E, D, DE, NH = 6250, 100000, 64, 32, 4
C = -(-N // P)
NP = P * C
K = 28
CHUNKS = 28
KT = K * CHUNKS
EP = P * KT
LOOPS = CHUNKS // 2
BIG = 1.0e30
REP = 4
ACC_ROWS = 2 * NP + P
E_ROWS = EP + 1 + P
B_ROWS = EP + NP
assert EP >= E and NP > N and KT % K == 0


class Link:

    def __init__(self, eng, sem, base=0):
        self.eng, self.sem, self.base, self.n = eng, sem, base, 0

    def __call__(self, ins):
        self.n += 1
        ins.then_inc(self.sem, 1)
        self.eng.wait_ge(self.sem, self.base + self.n)


def scratch(nc, name, shape, dtype=F32):
    return nc.sbuf_tensor(f"{name}_{nc.next_id()}", shape, dtype)


class Phase(dict):

    def __init__(self, nc, names, pairs, ctx):
        self.nc, self.ctx, self.opened = nc, ctx, ExitStack()
        self.sems = []
        for n in names.split():
            self.sems.append(ctx.enter_context(nc.semaphore(n)))
            self[n] = self.sems[-1]
        for n in pairs.split():
            two = [ctx.enter_context(nc.semaphore(f"{n}{i}")) for i in range(2)]
            self.sems += two
            self[n] = two

    def sbuf(self, name, shape, dtype=F32):
        return self.ctx.enter_context(scratch(self.nc, name, shape, dtype))

    def psum(self, name, shape):
        return self.ctx.enter_context(self.nc.psum_tensor(f"{name}_{self.nc.next_id()}", shape, F32))

    def block(self):
        return self.opened.enter_context(self.nc.Block())


@contextmanager
def phase(nc, names, pairs=""):
    with ExitStack() as ctx:
        s = Phase(nc, names, pairs, ctx)
        with s.opened:
            yield s
        with nc.Block() as block:
            @block.gpsimd
            def _(gp):
                gp.dma_reset()
                for h in s.sems:
                    gp.sem_clear(h)


def node_rows(dram):
    return dram.rearrange("(c p) w -> p c w", p=P)


def table_rows(dram):
    return dram.rearrange("(p c) w -> p c w", p=P)


def edge_rows(dram):
    return dram[0:EP, :].rearrange("(p k) w -> p k w", p=P)


def edge_rows_after(dram, n):
    return dram[n:EP + n, :].rearrange("(p k) w -> p k w", p=P)


def offset(ap):
    return bass.IndirectOffsetOnAxis(ap=ap, axis=0)


def bc(ap, n):
    return ap.unsqueeze(len(ap.shape)).to_broadcast([*ap.shape, n])


def mid(ap, n):
    return ap.unsqueeze(1).to_broadcast([ap.shape[0], n, ap.shape[1]])


def flat(ap):
    return ap.rearrange("p a b -> p (a b)")


def prepare(nc, g, a):
    with phase(nc, "loaded hist_done dve_link pool_link pe_done zeros_set zeroed ready", "onehot_ready onehot_used") as s:
        dst_i = s.sbuf("dst_i", [P, KT + 2], I32)
        dst_f = s.sbuf("dst_f", [P, KT + 2])
        lo_i = s.sbuf("lo_i", [P, KT], I32)
        lo_f = s.sbuf("lo_f", [P, KT])
        hi_f = s.sbuf("hi_f", [P, KT])
        src_i = s.sbuf("src_i", [P, KT], I32)
        typ_i = s.sbuf("typ_i", [P, KT], I32)
        work = s.sbuf("work", [P, KT])
        kpos = s.sbuf("kpos", [P, KT], I32)
        iota_i = s.sbuf("iota_i", [P, P], I32)
        pcol_i = s.sbuf("pcol_i", [P, 1], I32)
        ncol_i = s.sbuf("ncol_i", [P, C], I32)
        ncol = s.sbuf("ncol", [P, C])
        lo_b = s.sbuf("lo_b", [P, KT], BF16)
        hi_b = s.sbuf("hi_b", [P, KT], BF16)
        iota_w = s.sbuf("iota_w", [P, P, K], BF16)
        lo_hot = s.sbuf("lo_hot", [P, 2, P, K], BF16)
        hi_hot = s.sbuf("hi_hot", [P, 2, C, K], BF16)
        zero_hot = s.sbuf("zero_hot", [P, P], BF16)
        zeros = s.sbuf("zeros", [P, 1568])
        empty = s.sbuf("empty", [1, 72])
        count = s.sbuf("count", [P, C])
        nonempty = s.sbuf("nonempty", [P, C])
        sums = s.sbuf("sums", [P, 4, C])
        bnd = s.sbuf("bnd", [P, 8])
        gat_wT = s.sbuf("gat_wT", [D, D + 2 * D])
        gat_a = s.sbuf("gat_a", [D, 4])
        ps_hist = s.psum("ps_hist", [P, 512])
        ps_cum = s.psum("ps_cum", [P, 512])
        ps_tot = s.psum("ps_tot", [P, 512])
        ps_w = s.psum("ps_w", [P, 512])
        block = s.block()
        LOADS = 6

        @block.sync
        def _(sp):
            sp.dma_start(dst_i[:], a["dst_ext"]).then_inc(s["loaded"], 16)
            sp.dma_start(src_i[:], a["src_pad"]).then_inc(s["loaded"], 16)
            sp.dma_start(typ_i[:], a["type_pad"]).then_inc(s["loaded"], 16)
            sp.dma_start(g.x[:], node_rows(a["x_pad"])).then_inc(s["loaded"], 16)
            sp.dma_start(gat_wT[:], a["gat_wT"]).then_inc(s["loaded"], 16)
            sp.dma_start(gat_a[:], a["gat_a"]).then_inc(s["loaded"], 16)
            sp.dma_start(g.gat_w[:, 0, 0:D], a["gat_w_skip"]).then_inc(s["loaded"], 16)
            sp.dma_start(g.gat_w[0:D, 1, 0:D], a["gat_w_std"]).then_inc(s["loaded"], 16)
            sp.wait_ge(s["loaded"], 16 * (LOADS + 2))

        @block.scalar
        def _(act):
            act.wait_ge(s["zeros_set"], 1)
            act.wait_ge(s["loaded"], 16 * (LOADS + 2))
            act.dma_start(g.d_b64[0:EP, :].rearrange("(p k) w -> p (k w)", p=P).rearrange("p (r x) -> p r x", x=1568),
                          mid(zeros[:], KT * D // 1568)).then_inc(s["zeroed"], 16)
            n = 1
            for r in range(REP):
                act.dma_start(g.d_acc[r][0:2 * NP, :].rearrange("(p k) w -> p (k w)", p=P)
                              .rearrange("p (r x) -> p r x", x=1568),
                              mid(zeros[:], 2 * C * D // 1568)).then_inc(s["zeroed"], 16)
                act.dma_start(g.d_acc[r][2 * NP:, :], zeros[:, 0:D]).then_inc(s["zeroed"], 16)
                n += 2
            for d in (g.d_b1, g.d_b64, g.d_b96):
                act.dma_start(d[EP:EP + 2 * K, :], zeros[0:2 * K, 0:d.shape[1]]).then_inc(s["zeroed"], 16)
                n += 1
            for d in (g.d_e66, g.d_e72):
                w = d.shape[1]
                act.dma_start(d[EP + 1:, :], zeros[:, 0:w]).then_inc(s["zeroed"], 16)
                act.dma_start(d[EP:EP + 1, 0:w], empty[0:1, 72 - w:72]).then_inc(s["zeroed"], 16)
                n += 2
            act.wait_ge(s["zeroed"], 16 * n)

        @block.gpsimd
        def _(gp):
            gp.iota(iota_i[:], [[1, P]], base=0, channel_multiplier=0).then_inc(s["pool_link"], 1)
            gp.iota(pcol_i[:], [[0, 1]], base=0, channel_multiplier=1).then_inc(s["pool_link"], 1)
            gp.iota(kpos[:], [[1, KT]], base=0, channel_multiplier=KT).then_inc(s["pool_link"], 1)
            gp.iota(ncol_i[:], [[P, C]], base=0, channel_multiplier=1).then_inc(s["pool_link"], 1)

        @block.vector
        def _(v):
            link = Link(v, s["dve_link"])
            link(nc.vector.memset(empty[:], 0.0))
            link(nc.vector.memset(empty[0:1, 68:72], -BIG))
            nc.vector.memset(zeros[:], 0.0).then_inc(s["zeros_set"], 1)
            link(nc.vector.memset(zero_hot[:], 0.0))
            link(nc.vector.memset(g.ones[:], 1.0))
            v.wait_ge(s["pool_link"], 4)
            link(nc.vector.tensor_copy(g.iota[:], iota_i[:]))
            link(nc.vector.tensor_copy(g.pcol[:], pcol_i[:]))
            link(nc.vector.tensor_copy(ncol[:], ncol_i[:]))
            link(nc.vector.tensor_scalar(g.ident[:], g.iota[:], g.pcol[:, 0:1], None, ALU.is_equal))
            link(nc.vector.tensor_scalar(g.before[:], g.iota[:], g.pcol[:, 0:1], None, ALU.is_gt))
            link(nc.vector.tensor_scalar(g.after[:], g.iota[:], g.pcol[:, 0:1], None, ALU.is_lt))
            v.wait_ge(s["loaded"], 16 * (LOADS + 2))
            link(nc.vector.tensor_copy(dst_f[:], dst_i[:]))
            link(nc.vector.tensor_tensor(g.same[:, 0:KT], dst_f[:, 1:KT + 1], dst_f[:, 0:KT], ALU.is_equal))
            link(nc.vector.memset(g.same[:, KT:], 0.0))
            link(nc.vector.memset(g.src[:, KT:], 0))
            link(nc.vector.tensor_scalar(g.cut[:], g.same[:, 0:KT], -1.0, BIG, ALU.add, ALU.mult))
            link(nc.vector.tensor_copy(g.dst0_x[:], dst_i[:, 1:2]))
            link(nc.vector.tensor_scalar(lo_i[:], dst_i[:, 1:KT + 1], P - 1, None, ALU.bitwise_and))
            link(nc.vector.tensor_copy(lo_f[:], lo_i[:]))
            link(nc.vector.tensor_tensor(hi_f[:], dst_f[:, 1:KT + 1], lo_f[:], ALU.subtract))
            link(nc.vector.tensor_scalar(hi_f[:], hi_f[:], 1.0 / P, None, ALU.mult))
            link(nc.vector.tensor_copy(lo_b[:], lo_f[:]))
            link(nc.vector.tensor_copy(hi_b[:], hi_f[:]))
            link(nc.vector.tensor_copy(iota_w[:], bc(g.iota[:], K)))
            link(nc.vector.tensor_tensor(work[:], dst_f[:, 2:KT + 2], dst_f[:, 1:KT + 1], ALU.is_equal))
            link(nc.vector.scalar_tensor_tensor(work[:], work[:], 4.0 * EP, kpos[:], ALU.mult, ALU.add))
            link(nc.vector.tensor_reduce(bnd[:, 0:1], work[:], AX.X, ALU.min))
            link(nc.vector.tensor_scalar(bnd[:, 1:2], bnd[:, 0:1], 2.0 * EP, None, ALU.is_lt))
            link(nc.vector.tensor_tensor(bnd[:, 1:2], bnd[:, 1:2], g.same[:, 0:1], ALU.mult))
            link(nc.vector.tensor_scalar(bnd[:, 2:3], g.pcol[:], float(EP + 1), None, ALU.add))
            link(nc.vector.tensor_tensor(bnd[:, 3:4], bnd[:, 0:1], bnd[:, 2:3], ALU.subtract))
            link(nc.vector.tensor_tensor(bnd[:, 3:4], bnd[:, 3:4], bnd[:, 1:2], ALU.mult))
            link(nc.vector.tensor_tensor(bnd[:, 3:4], bnd[:, 3:4], bnd[:, 2:3], ALU.add))
            link(nc.vector.tensor_copy(g.idx_join[:], bnd[:, 3:4]))
            link(nc.vector.tensor_reduce(bnd[:, 4:5], g.same[:, 0:KT], AX.X, ALU.min))
            link(nc.vector.tensor_scalar(bnd[:, 5:6], bnd[:, 4:5], -1.0, BIG, ALU.add, ALU.mult))
            with v.Fori(0, LOOPS) as t:
                for b in range(2):
                    cols = bass.ds((2 * t + b) * K, K)
                    v.wait_ge(s["onehot_used"][b], t + 1)
                    nc.vector.tensor_tensor(lo_hot[:, b], iota_w[:], mid(lo_b[:, cols], P), ALU.is_equal)
                    nc.vector.tensor_tensor(hi_hot[:, b], iota_w[:, 0:C, :], mid(hi_b[:, cols], C),
                                            ALU.is_equal).then_inc(s["onehot_ready"][b], 1)
            def table_row(out, ids, lo, lo_f, hi_f):
                link(nc.vector.tensor_scalar(lo, ids, P - 1, None, ALU.bitwise_and))
                link(nc.vector.tensor_tensor(hi_f, ids, lo, ALU.subtract))
                link(nc.vector.tensor_scalar(lo_f, lo, float(C), None, ALU.mult))
                link(nc.vector.scalar_tensor_tensor(out, hi_f, 1.0 / P, lo_f, ALU.mult, ALU.add))

            for b in range(2):
                v.wait_ge(s["onehot_ready"][b], LOOPS)
            table_row(g.src[:, 0:KT], src_i[:], lo_i[:], lo_f[:], hi_f[:])
            table_row(g.dst0[:], dst_i[:, 1:2], lo_i[:, 0:1], lo_f[:, 0:1], hi_f[:, 0:1])
            link(nc.vector.scalar_tensor_tensor(g.key[:], typ_i[:], float(NP), g.src[:, 0:KT], ALU.mult, ALU.add))
            v.wait_ge(s["hist_done"], 1)
            link(nc.vector.tensor_copy(count[:], ps_hist[:, 0:C]))
            nc.vector.tensor_copy(sums[:, 0], count[:]).then_inc(s["ready"], 1)
            link(nc.vector.tensor_scalar(nonempty[:], count[:], 0.0, None, ALU.is_gt))
            v.wait_ge(s["pe_done"], 1)
            link(nc.vector.tensor_copy(sums[:, 1], ps_tot[:, 0:C]))
            link(nc.vector.tensor_tensor_scan(sums[:, 2], g.ones[:, 0:C], sums[:, 1], 0.0,
                                              ALU.mult, ALU.add))
            link(nc.vector.tensor_tensor(sums[:, 2], sums[:, 2], sums[:, 1], ALU.subtract))
            link(nc.vector.tensor_tensor(sums[:, 3], sums[:, 2], ps_cum[:, 0:C], ALU.add))
            link(nc.vector.tensor_tensor(sums[:, 1], sums[:, 3], count[:], ALU.add))
            link(nc.vector.tensor_scalar(sums[:, 1], sums[:, 1], -1.0 - EP, None, ALU.add))
            link(nc.vector.tensor_tensor(sums[:, 1], sums[:, 1], nonempty[:], ALU.mult))
            link(nc.vector.tensor_scalar(sums[:, 1], sums[:, 1], float(EP), None, ALU.add))
            link(nc.vector.tensor_copy(g.idx_last[:], sums[:, 1]))
            link(nc.vector.tensor_scalar(ncol[:], ncol[:], float(EP), None, ALU.add))
            link(nc.vector.tensor_tensor(sums[:, 3], sums[:, 3], ncol[:], ALU.subtract))
            link(nc.vector.tensor_tensor(sums[:, 3], sums[:, 3], nonempty[:], ALU.mult))
            link(nc.vector.tensor_tensor(sums[:, 3], sums[:, 3], ncol[:], ALU.add))
            link(nc.vector.tensor_copy(g.idx_first[:], sums[:, 3]))
            v.wait_ge(s["pe_done"], 2)
            link(nc.vector.tensor_copy(g.pass_cut[:], ps_tot[0:68, 128:256]))
            link(nc.vector.tensor_copy(g.gat_w[:, 0, D:D + 2], ps_w[:, 0:2]))
            link(nc.vector.tensor_copy(g.gat_w[0:D, 1, D:D + 2], ps_w[0:D, 2:4]))

        @block.tensor
        def _(pe):
            for b in range(2):
                pe.sem_inc(s["onehot_used"][b], 1)
            pe.wait_ge(s["dve_link"], 4)
            nc.tensor.matmul(ps_hist[:, 0:C], zero_hot[:], zero_hot[:, 0:C], start=True, stop=False)
            with pe.Fori(0, LOOPS) as t:
                for b in range(2):
                    pe.wait_ge(s["onehot_ready"][b], t + 1)
                    for k in range(K):
                        mm = nc.tensor.matmul(ps_hist[:, 0:C], lo_hot[:, b, :, k], hi_hot[:, b, :, k],
                                              start=False, stop=False)
                    mm.then_inc(s["onehot_used"][b], 1)
            nc.tensor.matmul(ps_hist[:, 0:C], zero_hot[:], zero_hot[:, 0:C],
                             start=False, stop=True).then_inc(s["hist_done"], 1)
            pe.wait_ge(s["ready"], 1)
            nc.tensor.matmul(ps_cum[:, 0:C], g.before[:], sums[:, 0], start=True, stop=True)
            nc.tensor.matmul(ps_tot[:, 0:C], g.ones[:], sums[:, 0], start=True, stop=True)
            nc.tensor.matmul(ps_tot[0:68, 128:256], bnd[:, 5:6].to_broadcast([P, 68]), g.ident[:],
                             start=True, stop=True).then_inc(s["pe_done"], 1)
            nc.tensor.matmul(ps_w[:, 0:2], gat_wT[:, 0:2 * D], gat_a[:, 0:2], start=True, stop=True)
            nc.tensor.matmul(ps_w[0:D, 2:4], gat_wT[:, 2 * D:], gat_a[:, 2:4],
                             start=True, stop=True).then_inc(s["pe_done"], 1)


def layer0_edges(nc, g, a):
    BANK = 8
    SG = [(k, min(k + BANK, K)) for k in range(0, K, BANK)]
    KG = [(k, k + 4) for k in range(0, K, 4)]
    SG_BANKS = len(SG)
    with phase(nc, "pool_steps spread_link dve_link keys_f keys_turned pairs_ready  sums_copied "
               "wide_zeroed zeros_set b_turned x_spread seeded seed_taken loaded shifted exp_done",
               "b_loaded spread_done added0 added1 added2 added3 idx_ready pairs_used") as s:
        b_rows = s.sbuf("b_rows", [P, 2, K, D])
        b_f = s.sbuf("b_f", [P, 2, D, K])
        same_w = s.sbuf("same_w", [P, 2, D, K], BF16)
        key_f = s.sbuf("key_f", [P, 2, K])
        pairs = s.sbuf("pairs", [P, 2, K, P])
        earlier = s.sbuf("earlier", [P, K, P])
        again = s.sbuf("again", [P, K])
        idx_f = s.sbuf("idx_f", [P, K])
        idx = s.sbuf("idx", [P, 2, K], I32)
        sums = s.sbuf("sums", [P, 2, K, D])
        spare = s.sbuf("spare", [P, 1])
        relw = s.sbuf("relw", [P, 4, D])
        att_b = s.sbuf("att_b", [P, 1])
        prod = s.sbuf("prod", [P, C, D])
        rel_prod = s.sbuf("rel_prod", [P, D])
        rel = s.sbuf("rel", [P, 2])
        dot = s.sbuf("dot", [P, C])
        zeros = s.sbuf("zeros", [P, KT])
        prime = s.sbuf("prime", [1, 2 * REP])
        ps_key0 = s.psum("ps_key0", [P, 512])
        ps_key1 = s.psum("ps_key1", [P, 512])
        ps_sum = s.psum("ps_sum", [P, SG_BANKS, 512])
        block = s.block()
        ps_key = (ps_key0, ps_key1)
        added = list(zip(s["added0"], s["added1"], s["added2"], s["added3"]))
        PER = K // REP
        LINKS = 6

        @block.sync
        def _(sp):
            sp.dma_start(relw[:], a["rel_rows"].partition_broadcast(P)).then_inc(s["loaded"], 16)
            sp.dma_start(att_b[:], a["att_b"].partition_broadcast(P)).then_inc(s["loaded"], 16)
            sp.wait_ge(s["x_spread"], 16 * C)
            sp.dma_start(b_rows[:, 0], edge_rows(g.d_b64)[:, 0:K, :]).then_inc(s["b_loaded"][0], 16)
            with sp.Fori(0, LOOPS) as t:
                for b in range(2):
                    cols = bass.ds((2 * t + b) * K, K)
                    sp.wait_ge(s["b_turned"], 2 * t + b + 1)
                    sp.dma_start(b_rows[:, 1 - b], edge_rows_after(g.d_b64, K)[:, cols, :]).then_inc(s["b_loaded"][1 - b], 16)

        @block.vector
        def _(v):
            nc.vector.memset(same_w[:, :, :, 0:1], 0.0).then_inc(s["zeros_set"], 1)
            nc.vector.memset(zeros[:], 0.0).then_inc(s["zeros_set"], 1)
            nc.vector.tensor_scalar(spare[:], g.pcol[:], float(2 * NP), None, ALU.add).then_inc(s["spread_link"], 1)
            v.wait_ge(s["spread_link"], 1)
            pre = Link(v, s["spread_link"], 1)
            v.wait_ge(s["loaded"], 32)
            pre(nc.vector.tensor_tensor(prod[:], g.x[:], mid(relw[:, 0], C), ALU.mult))
            pre(nc.vector.tensor_reduce(dot[:], prod[:], AX.X, ALU.add))
            for ty in range(2):
                pre(nc.vector.tensor_tensor(rel_prod[:], relw[:, 2 + ty], relw[:, 1], ALU.mult))
                pre(nc.vector.tensor_reduce(rel[:, ty:ty + 1], rel_prod[:], AX.X, ALU.add))
                pre(nc.vector.tensor_tensor(rel[:, ty:ty + 1], rel[:, ty:ty + 1], att_b[:], ALU.add))
                nc.vector.tensor_scalar(g.attention[:, ty], dot[:], rel[:, ty:ty + 1], -1.0,
                                        ALU.add, ALU.mult).then_inc(s["shifted"], 1)
            v.wait_ge(s["exp_done"], 1)
            pre(nc.vector.tensor_scalar(flat(g.attention[:]), flat(g.attention[:]), 1.0, None, ALU.add))
            pre(nc.vector.reciprocal(flat(g.attention[:]), flat(g.attention[:])))
            v.wait_ge(s["seeded"], 16)
            v.sem_inc(s["seed_taken"], 1)
            with v.Fori(0, LOOPS) as t:
                for b in range(2):
                    chunk = 2 * t + b
                    link = Link(v, s["dve_link"], chunk * LINKS)
                    cols = bass.ds(chunk * K, K)
                    v.wait_ge(s["pairs_used"][b], t + 1)
                    nc.vector.tensor_copy(key_f[:, b], g.key[:, cols]).then_inc(s["keys_f"], 1)
                    v.wait_ge(s["keys_f"], chunk + 1)
                    for i, (k0, k1) in enumerate(KG):
                        v.wait_ge(s["keys_turned"], len(KG) * chunk + i + 1)
                        pr = nc.vector.tensor_tensor(
                            pairs[:, b, k0:k1, :], ps_key[i % 2][:].rearrange("p (k e) -> p k e", e=P),
                            bc(key_f[:, b, k0:k1], P), ALU.is_equal)
                        pr.then_inc(s["pairs_ready"], 1)
                    v.wait_ge(s["b_turned"], chunk + 2)
                    first = b_f[:, b, :, 0]
                    link(nc.vector.scalar_tensor_tensor(first, g.seed[:, 0:D], g.same[:, bass.ds(chunk * K, 1)], first,
                                                        ALU.mult, ALU.add))
                    part = b_f[:, b].rearrange("p f k -> p (f k)")
                    nc.vector.tensor_tensor_scan(part, same_w[:, b].rearrange("p f k -> p (f k)"), part, 0.0,
                                                 ALU.mult, ALU.add).then_inc(s["spread_done"][b], 1)
                    v.wait_ge(s["spread_done"][b], t + 1)
                    nc.vector.tensor_copy(g.seed[:, 0:D], b_f[:, b, :, K - 1]).then_inc(s["seed_taken"], 1)
                    v.wait_ge(s["seed_taken"], chunk + 2)
                    v.wait_ge(s["pairs_ready"], len(KG) * (chunk + 1))
                    link(nc.vector.tensor_tensor(earlier[:], pairs[:, b], mid(g.after[:], K), ALU.mult))
                    link(nc.vector.tensor_reduce(again[:], earlier[:], AX.X, ALU.max))
                    link(nc.vector.tensor_scalar(idx_f[:], key_f[:, b], spare[:, 0:1], -1.0, ALU.subtract, ALU.mult))
                    link(nc.vector.tensor_tensor(idx_f[:], idx_f[:], again[:], ALU.mult))
                    link(nc.vector.tensor_tensor(idx_f[:], idx_f[:], key_f[:, b], ALU.add))
                    for r in range(REP):
                        v.wait_ge(added[b][r], 16 * (PER * t + 1))
                    nc.vector.tensor_copy(idx[:, b], idx_f[:]).then_inc(s["idx_ready"][b], 1)
                    assert link.n == LINKS, link.n

        @block.tensor
        def _(pe):
            for b in range(2):
                pe.sem_inc(s["pairs_used"][b], 1)
            with pe.Fori(0, LOOPS) as t:
                for b in range(2):
                    chunk = 2 * t + b
                    pe.wait_ge(s["keys_f"], chunk + 1)
                    for i, (k0, k1) in enumerate(KG):
                        if i >= 2:
                            pe.wait_ge(s["pairs_ready"], len(KG) * chunk + i - 1)
                        for k in range(k0, k1):
                            mm = nc.tensor.matmul(ps_key[i % 2][:, (k - k0) * P:(k - k0 + 1) * P],
                                                  key_f[:, b, k:k + 1].to_broadcast([P, P]), g.ident[:],
                                                  start=True, stop=True)
                        mm.then_inc(s["keys_turned"], 1)
                    pe.wait_ge(s["pairs_ready"], len(KG) * (chunk + 1))
                    pe.wait_ge(s["spread_done"][b], t + 1)
                    pe.wait_ge(s["sums_copied"], chunk + 1)
                    for i, (k0, k1) in enumerate(SG):
                        for k in range(k0, k1):
                            mm = nc.tensor.matmul(ps_sum[:, i, (k - k0) * D:(k - k0 + 1) * D],
                                                  pairs[:, b, k, :], b_f[:, b, :, k], start=True, stop=True)
                    mm.then_inc(s["pairs_used"][b], 1)

        @block.scalar
        def _(act):
            act.sem_inc(s["sums_copied"], 1)
            act.sem_inc(s["b_turned"], 1)
            def turn_b(chunk, b, round_):
                nc.scalar.copy(same_w[:, b, :, 1:], g.same[:, bass.ds(chunk * K + 1, K - 1)].unsqueeze(1)
                               .to_broadcast([P, D, K - 1]))
                act.wait_ge(s["b_loaded"][b], 16 * (round_ + 1))
                nc.scalar.copy(b_f[:, b], b_rows[:, b].rearrange("p k f -> p f k")).then_inc(s["b_turned"], 1)

            act.wait_ge(s["shifted"], 2)
            nc.scalar.activation(flat(g.attention[:]), flat(g.attention[:]), ACT.Exp).then_inc(s["exp_done"], 1)
            act.wait_ge(s["zeros_set"], 1)
            turn_b(0, 0, 0)
            act.wait_ge(s["zeros_set"], 2)
            act.dma_start(g.d_b1[0:EP, :].rearrange("(p k) w -> p (k w)", p=P), zeros[:, 0:KT]).then_inc(s["wide_zeroed"], 16)
            with act.Fori(0, LOOPS) as t:
                for b in range(2):
                    act.wait_ge(s["pairs_used"][1 - b], t + b + 1)
                    act.wait_ge(s["seed_taken"], 2 * t + b + 1)
                    turn_b(2 * t + b + 1, 1 - b, t + b)
                    act.wait_ge(s["pairs_used"][b], t + 2)
                    for r in range(REP):
                        act.wait_ge(added[b][r], 16 * (PER * t + 1))
                    for i, (k0, k1) in enumerate(SG):
                        cp = nc.scalar.copy(flat(sums[:, b, k0:k1, :]), ps_sum[:, i, 0:(k1 - k0) * D])
                    cp.then_inc(s["sums_copied"], 1)
            act.wait_ge(s["wide_zeroed"], 16)

        @block.gpsimd
        def _(gp):
            for b in range(2):
                for r in range(REP):
                    gp.dma_start(prime[0:1, REP * b + r:REP * b + r + 1], g.d_x[0:1, 0:1]).then_inc(added[b][r], 16)
            gp.indirect_dma_start(g.seed[:, 0:D], None, g.d_x[:, :], offset(g.dst0_x[:])).then_inc(s["seeded"], 16)
            for c in range(C):
                gp.indirect_dma_start(g.d_b64[:, :], offset(g.idx_first[:, c:c + 1]),
                                      g.x[:, c, :], None).then_inc(s["x_spread"], 16)
            with gp.Fori(0, LOOPS) as t:
                for b in range(2):
                    chunk = 2 * t + b
                    gp.wait_ge(s["idx_ready"][b], t + 1)
                    gp.wait_ge(s["sums_copied"], chunk + 2)
                    for k in range(K):
                        r = k % REP
                        if k >= REP:
                            gp.wait_ge(added[b][r], 16 * (PER * t + k // REP + 1))
                        else:
                            gp.wait_ge(added[1 - b][r], 16 * (PER * (t + b) + 1))
                        gp.sem_inc(s["pool_steps"], 1)
                        gp.indirect_dma_start(g.d_acc[r][:, :], offset(idx[:, b, k:k + 1]), sums[:, b, k, :], None,
                                              compute_op=ALU.add).then_inc(added[b][r], 16)
            for r in range(REP):
                for b in range(2):
                    gp.wait_ge(added[b][r], 16 * (PER * LOOPS + 1))


def edges(nc, g, kind, a=None, update=False, clear=None):
    H = NH if kind == "multi" else 1
    FZ = D + H
    R = FZ + H
    table = {"gat": g.d_t66, "dot": g.d_t128, "multi": g.d_t160 if update else g.d_t128}[kind]
    TW = table.shape[1]
    v0 = TW - D if kind != "gat" else 0
    k0 = TW - 2 * D
    spread = {"gat": g.d_b1, "dot": g.d_b64, "multi": g.d_b96 if update else g.d_b64}[kind]
    BW = spread.shape[1]
    seed0 = D + 1 if kind == "gat" else 0
    states = g.d_e72 if kind == "multi" else g.d_e66
    multi = kind == "multi"
    EW = DE if multi else 1
    G4 = K // 4
    HALVES = ((0, 4), (4, G4))
    turns = 2 if update else 1
    PARTS = 4 if update else 1
    PW = BW // PARTS
    with phase(nc, "pool_steps sp_steps we_read state_init dve_link logits_done exps_done loaded e_turned e_copied "
                   "e_product we_product pre_ready gelu_done centred squared var_ready rooted tail_saved "
                   "b_loaded b_turned spread_done factors_wide states_done states_turned zeros_set",
               "idx_ready e_loaded gathered rows_used stored e_ready e_stored") as s:
        idx = s.sbuf("idx", [P, 2, K], I32)
        rows = s.sbuf("rows", [P, 2, K, TW])
        b_rows = s.sbuf("b_rows", [P, K, BW])
        b_f = s.sbuf("b_f", [P, 2, BW, K])
        same_w = s.sbuf("same_w", [P, 2, BW, K], BF16)
        values = s.sbuf("values", [P, 2, R, K])
        factors_w = s.sbuf("factors_w", [P, FZ, K])
        state = s.sbuf("state", [P, 2, K, R])
        given = s.sbuf("given", [P, FZ])
        maxima = s.sbuf("maxima", [P, H, K + 1])
        logits = s.sbuf("logits", [P, H, K])
        factors = s.sbuf("factors", [P, 2, H, K])
        prod = s.sbuf("prod", [P, K, D if kind != "gat" else 1])
        e_rows = s.sbuf("e_rows", [P, 2, K, EW])
        e_T = s.sbuf("e_T", [P, G4 if multi else 1, P])
        pre = s.sbuf("pre", [P, K, EW])
        sq = s.sbuf("sq", [P, K, EW])
        stat = s.sbuf("stat", [P, 2, K])
        w_em = s.sbuf("w_em", [P, P if update else 1])
        w_e = s.sbuf("w_e", [P, 16])
        gs = s.sbuf("gs", [P, 2, DE])
        prime = s.sbuf("prime", [1, 4])
        zeros = s.sbuf("zeros", [P, K if clear is not None else 1, 96])
        ps_eT = s.psum("ps_eT", [P, 2, 512])
        ps_em = s.psum("ps_em", [P, 2, 512])
        ps_we = s.psum("ps_we", [P, 512])
        block = s.block()

        def e_columns(b, q):
            return e_rows[:, b, 4 * q:4 * q + 4, :].rearrange("p k f -> p (k f)")

        @block.sync
        def _(sp):
            if multi:
                sp.dma_start(w_e[:], a["w_e"]).then_inc(s["loaded"], 16)
                if update:
                    sp.dma_start(w_em[:], a["w_em"]).then_inc(s["loaded"], 16)
                    sp.dma_start(gs[:], a["e_norm"].partition_broadcast(P)).then_inc(s["loaded"], 16)
            if clear is not None:
                sp.wait_ge(s["zeros_set"], 1)
            for c in range(2):
                if c:
                    sp.wait_ge(s["b_turned"], c)
                sp.dma_start(b_rows[:], edge_rows(spread)[:, c * K:c * K + K, :]).then_inc(s["b_loaded"], 16)
            with sp.Fori(0, LOOPS) as t:
                for b in range(2):
                    chunk = 2 * t + b
                    cols = bass.ds(chunk * K, K)
                    if multi:
                        if update:
                            sp.wait_ge(s["e_stored"][b], 16 * (t + 1))
                        sp.sem_inc(s["sp_steps"], 1)
                        sp.dma_start(e_rows[:, b], edge_rows(g.d_edge)[:, cols, :]).then_inc(s["e_loaded"][b], 16)
                    sp.wait_ge(s["b_turned"], chunk + 2)
                    sp.dma_start(b_rows[:], edge_rows_after(spread, 2 * K)[:, cols, :]).then_inc(s["b_loaded"], 16)
                    if clear is not None:
                        sp.dma_start(edge_rows(clear)[:, cols, :], zeros[:]).then_inc(s["e_stored"][b], 16)
                    if kind == "dot":
                        sp.dma_start(edge_rows(g.d_edge)[:, cols, :],
                                     edge_rows(a["edge_pad"])[:, cols, :]).then_inc(s["e_stored"][b], 16)
            if kind == "dot" or clear is not None:
                for b in range(2):
                    sp.wait_ge(s["e_stored"][b], 16 * LOOPS)
            if update:
                sp.wait_ge(s["e_stored"][0], 16 * (LOOPS + 1))
                sp.dma_start(e_rows[:, 0], edge_rows(g.d_edge)[:, 0:K, :]).then_inc(s["e_loaded"][0], 16)

        @block.gpsimd
        def _(gp):
            with gp.Fori(0, LOOPS) as t:
                for b in range(2):
                    gp.wait_ge(s["rows_used"][b], t + 1)
                    gp.wait_ge(s["idx_ready"][b], t + 1)
                    gp.sem_inc(s["pool_steps"], 1)
                    for k in range(K):
                        gp.indirect_dma_start(rows[:, b, k, :], None, table[:, :],
                                              offset(idx[:, b, k:k + 1])).then_inc(s["gathered"][b], 16)

        @block.scalar
        def _(act):
            def turn_e(n):
                for half, (q0, q1) in enumerate(HALVES):
                    act.wait_ge(s["e_turned"], 2 * n + half + 1)
                    nc.scalar.copy(flat(e_T[:, q0:q1, :]), ps_eT[:, half, 0:(q1 - q0) * P]).then_inc(s["e_copied"], 1)

            def widen_mask(b, start):
                nc.scalar.copy(same_w[:, b, :, 1:], g.same[:, bass.ds(start + 1, K - 1)].unsqueeze(1)
                               .to_broadcast([P, BW, K - 1]))

            def turn_b(chunk, b):
                act.wait_ge(s["b_loaded"], 16 * (chunk + 1))
                nc.scalar.copy(b_f[:, b], b_rows[:].rearrange("p k f -> p f k")).then_inc(s["b_turned"], 1)

            for b in range(2):
                act.dma_start(prime[0:1, b:b + 1], g.d_x[0:1, 0:1]).then_inc(s["stored"][b], 16)
                if update:
                    act.dma_start(prime[0:1, 2 + b:3 + b], g.d_x[0:1, 0:1]).then_inc(s["e_stored"][b], 16)
            act.wait_ge(s["state_init"], 1)
            for b in range(2):
                widen_mask(b, b * K)
                turn_b(b, b)
            if update:
                turn_e(0)
            with act.Fori(0, LOOPS) as t:
                for b in range(2):
                    chunk = 2 * t + b
                    cols = bass.ds(chunk * K, K)
                    if multi and not update:
                        turn_e(chunk)
                    if update:
                        act.wait_ge(s["pre_ready"], chunk + 1)
                        nc.scalar.activation(flat(pre[:]), flat(pre[:]), ACT.Gelu_apprx_tanh).then_inc(s["gelu_done"], 1)
                        act.wait_ge(s["centred"], chunk + 1)
                        nc.scalar.activation(flat(sq[:]), flat(pre[:]), ACT.Square).then_inc(s["squared"], 1)
                        act.wait_ge(s["var_ready"], chunk + 1)
                        nc.scalar.activation(stat[:, 1], stat[:, 1], ACT.Sqrt).then_inc(s["rooted"], 1)
                        turn_e(2 * chunk + 1)
                        act.wait_ge(s["e_ready"][b], t + 1)
                        act.dma_start(edge_rows(g.d_edge)[:, cols, :], e_rows[:, b]).then_inc(s["e_stored"][b], 16)
                    act.wait_ge(s["spread_done"], (PARTS + 1) * (chunk + 1))
                    widen_mask(b, (chunk + 2) * K)
                    act.wait_ge(s["logits_done"], chunk + 1)
                    f = factors[:].rearrange("p a h k -> p (a h k)")
                    nc.scalar.activation(f, f, ACT.Exp).then_inc(s["exps_done"], 1)
                    act.wait_ge(s["exps_done"], chunk + 1)
                    for h in range(H):
                        nc.scalar.copy(factors_w[:, h * D // H:(h + 1) * D // H, 1:],
                                       mid(factors[:, 0, h, 1:], D // H))
                    nc.scalar.copy(factors_w[:, D:FZ, 1:], factors[:, 0, :, 1:]).then_inc(s["factors_wide"], 1)
                    if update:
                        turn_e(2 * chunk + 2)
                    act.wait_ge(s["spread_done"], (PARTS + 1) * (chunk + 1) + 1)
                    turn_b(chunk + 2, b)
                    act.wait_ge(s["stored"][b], 16 * (t + 1))
                    act.wait_ge(s["states_done"], chunk + 1)
                    nc.scalar.copy(state[:, b], values[:, b].rearrange("p f k -> p k f")).then_inc(s["states_turned"], 1)
                    act.wait_ge(s["states_turned"], chunk + 3)
                    act.dma_start(edge_rows(states)[:, cols, :], state[:, b]).then_inc(s["stored"][b], 16)
            for b in range(2):
                act.wait_ge(s["stored"][b], 16 * (LOOPS + 1))
                if update:
                    act.wait_ge(s["e_stored"][b], 16 * (LOOPS + 1))

        @block.tensor
        def _(pe):
            if not multi:
                return
            pe.wait_ge(s["loaded"], 16 * (3 if update else 1))

            def turn(n, b):
                for half, (q0, q1) in enumerate(HALVES):
                    for q in range(q0, q1):
                        mm = nc.tensor.transpose(ps_eT[:, half, (q - q0) * P:(q - q0 + 1) * P],
                                                 e_columns(b, q), g.ident[:])
                    mm.then_inc(s["e_turned"], 1)

            def old_product(chunk, b, round_, again=True):
                pe.wait_ge(s["e_loaded"][b], 16 * (round_ + 1))
                turn(2 * chunk, b)
                if again:
                    pe.wait_ge(s["pre_ready"], chunk)
                for q in range(G4):
                    if q % 4 == 0:
                        pe.wait_ge(s["e_copied"], 4 * chunk + q // 4 + 1)
                    mm = nc.tensor.matmul(ps_em[:, q // 4, (q % 4) * P:(q % 4 + 1) * P], e_T[:, q, :],
                                          w_em[:], start=True, stop=True)
                mm.then_inc(s["e_product"], 1)

            if update:
                old_product(0, 0, 0, False)
            with pe.Fori(0, LOOPS) as t:
                for b in range(2):
                    chunk = 2 * t + b
                    if update:
                        pe.wait_ge(s["e_product"], chunk + 1)
                        pe.wait_ge(s["e_ready"][b], t + 1)
                        turn(2 * chunk + 1, b)
                    else:
                        pe.wait_ge(s["e_loaded"][b], 16 * (t + 1))
                        turn(chunk, b)
                    pe.wait_ge(s["we_read"], chunk + 1)
                    for q in range(G4):
                        if q % 4 == 0:
                            pe.wait_ge(s["e_copied"], 2 * (turns * chunk + turns - 1) + q // 4 + 1)
                        mm = nc.tensor.matmul(ps_we[:, q * 16:(q + 1) * 16], e_T[:, q, :], w_e[:],
                                              start=True, stop=True)
                    mm.then_inc(s["we_product"], 1)
                    if update:
                        old_product(chunk + 1, 1 - b, t + b)

        LINKS = {"gat": 6, "dot": 7, "multi": 13 if update else 6}[kind]

        @block.vector
        def _(v):
            for b in range(2):
                nc.vector.tensor_copy(idx[:, b], g.src[:, b * K:b * K + K]).then_inc(s["idx_ready"][b], 1)
            for b in range(2):
                v.sem_inc(s["rows_used"][b], 1)
            if clear is not None:
                nc.vector.memset(zeros[:], 0.0).then_inc(s["zeros_set"], 1)
            nc.vector.memset(maxima[:], -BIG)
            nc.vector.memset(values[:, 1], 0.0)
            nc.vector.memset(factors_w[:, :, 0:1], 0.0)
            nc.vector.memset(same_w[:, :, :, 0:1], 0.0).then_inc(s["state_init"], 1)
            for b in range(2):
                v.sem_inc(s["states_turned"], 1)
            v.sem_inc(s["we_read"], 1)
            v.wait_ge(s["state_init"], 1)
            if update:
                v.wait_ge(s["loaded"], 48)

            def spread_part(chunk, b, start, i, before):
                if i == 0:
                    v.wait_ge(s["b_turned"], chunk + 1)
                    first = b_f[:, b, :, 0]
                    nc.vector.scalar_tensor_tensor(first, before, g.same[:, bass.ds(start, 1)], first,
                                                   ALU.mult, ALU.add).then_inc(s["spread_done"], 1)
                    v.wait_ge(s["spread_done"], (PARTS + 1) * chunk + 1)
                part = b_f[:, b, i * PW:(i + 1) * PW, :].rearrange("p f k -> p (f k)")
                mask = same_w[:, b, i * PW:(i + 1) * PW, :].rearrange("p f k -> p (f k)")
                nc.vector.tensor_tensor_scan(part, mask, part, 0.0, ALU.mult, ALU.add).then_inc(s["spread_done"], 1)

            for i in range(PARTS):
                spread_part(0, 0, 0, i, g.seed[:, seed0:seed0 + BW])
            with v.Fori(0, LOOPS) as t:
                for b in range(2):
                    chunk = 2 * t + b
                    link = Link(v, s["dve_link"], chunk * LINKS)
                    G, B, V = rows[:, b], b_f[:, b].rearrange("p f k -> p k f"), values[:, b]
                    cut_c = g.cut[:, bass.ds(chunk * K, K)]

                    def spread_next(i):
                        spread_part(chunk + 1, 1 - b, (chunk + 1) * K, i, b_f[:, b, :, K - 1])

                    v.wait_ge(s["spread_done"], (PARTS + 1) * (chunk + 1))
                    v.wait_ge(s["gathered"][b], 16 * K * (t + 1))
                    nc.vector.tensor_copy(idx[:, b], g.src[:, bass.ds((chunk + 2) * K, K)]).then_inc(s["idx_ready"][b], 1)
                    if update:
                        e = e_rows[:, b]
                        link(nc.vector.tensor_tensor(pre[:], G[:, :, 0:DE], B[:, :, D:D + DE], ALU.add))
                        v.wait_ge(s["e_product"], chunk + 1)
                        nc.vector.tensor_tensor(flat(pre[:]), flat(pre[:]),
                                                ps_em[:].rearrange("p a x -> p (a x)")[:, 0:K * DE],
                                                ALU.add).then_inc(s["pre_ready"], 1)
                        spread_next(0)
                        spread_next(1)
                        v.wait_ge(s["gelu_done"], chunk + 1)
                        link(nc.vector.tensor_tensor(pre[:], pre[:], e, ALU.add))
                        link(nc.vector.tensor_reduce(stat[:, 0], pre[:], AX.X, ALU.add))
                        nc.vector.scalar_tensor_tensor(pre[:], bc(stat[:, 0], DE), -1.0 / DE, pre[:],
                                                       ALU.mult, ALU.add).then_inc(s["centred"], 1)
                        spread_next(2)
                        v.wait_ge(s["squared"], chunk + 1)
                        link(nc.vector.tensor_reduce(stat[:, 1], sq[:], AX.X, ALU.add))
                        nc.vector.tensor_scalar(stat[:, 1], stat[:, 1], 1.0 / DE, 1e-5, ALU.mult, ALU.add).then_inc(s["var_ready"], 1)
                        v.wait_ge(s["centred"], chunk + 1)
                        link(nc.vector.tensor_tensor(pre[:], pre[:], mid(gs[:, 0], K), ALU.mult))
                        v.wait_ge(s["rooted"], chunk + 1)
                        link(nc.vector.reciprocal(stat[:, 1], stat[:, 1]))
                        link(nc.vector.tensor_tensor(pre[:], pre[:], bc(stat[:, 1], DE), ALU.mult))
                        nc.vector.tensor_tensor(e, pre[:], mid(gs[:, 1], K), ALU.add).then_inc(s["e_ready"][b], 1)
                    if kind == "gat":
                        link(nc.vector.tensor_tensor(logits[:, 0], G[:, :, D], B[:, :, 0], ALU.add))
                        spread_next(0)
                        link(nc.vector.scalar_tensor_tensor(logits[:, 0], logits[:, 0], 0.2, logits[:, 0], ALU.mult, ALU.max))
                    else:
                        link(nc.vector.tensor_tensor(prod[:], G[:, :, k0:k0 + D], B[:, :, 0:D], ALU.mult))
                        link(nc.vector.tensor_reduce(logits[:].rearrange("p h k -> p k h"),
                                                     prod[:].rearrange("p k (h d) -> p k h d", h=H), AX.X, ALU.add))
                        if kind == "dot":
                            link(nc.vector.scalar_tensor_tensor(logits[:, 0], logits[:, 0], 0.2, logits[:, 0],
                                                                ALU.mult, ALU.max))
                    if multi:
                        v.wait_ge(s["we_product"], chunk + 1)
                        nc.vector.scalar_tensor_tensor(
                            logits[:], logits[:], 0.25, ps_we[:, 0:K * NH].rearrange("p (k h) -> p h k", h=NH),
                            ALU.mult, ALU.add).then_inc(s["we_read"], 1)
                        v.wait_ge(s["we_read"], chunk + 2)
                    for h in range(H):
                        last = nc.vector.tensor_tensor_scan(maxima[:, h, 1:], cut_c, logits[:, h], maxima[:, h, 0:1],
                                                            ALU.add, ALU.max)
                    link(last)
                    nc.vector.tensor_tensor(factors[:, 1], logits[:], maxima[:, :, 1:], ALU.subtract)
                    link(nc.vector.tensor_tensor(factors[:, 0], maxima[:, :, 0:K], mid(cut_c, H), ALU.add))
                    nc.vector.tensor_tensor(factors[:, 0], factors[:, 0], maxima[:, :, 1:], ALU.subtract).then_inc(s["logits_done"], 1)
                    if kind != "gat":
                        spread_next(PARTS - 1)
                    v.wait_ge(s["logits_done"], chunk + 1)
                    v.wait_ge(s["states_turned"], chunk + 1)
                    nc.vector.tensor_copy(V[:, FZ:R, :], maxima[:, :, 1:])
                    nc.vector.tensor_copy(maxima[:, :, 0:1], maxima[:, :, K:K + 1])
                    v.wait_ge(s["exps_done"], chunk + 1)
                    weights = factors[:, 1].unsqueeze(2).to_broadcast([P, H, D // H, K])
                    nc.vector.tensor_copy(V[:, D:FZ, :], factors[:, 1])
                    nc.vector.tensor_tensor(V[:, 0:D, :].rearrange("p (h d) k -> p h d k", h=H),
                                            G[:, :, v0:v0 + D].rearrange("p k (h d) -> p h d k", h=H),
                                            weights, ALU.mult).then_inc(s["rows_used"][b], 1)
                    before = values[:, 1 - b, 0:FZ, K - 1]
                    nc.vector.tensor_tensor(given[:, 0:D].rearrange("p (h d) -> p h d", h=H),
                                            before[:, 0:D].rearrange("p (h d) -> p h d", h=H),
                                            bc(factors[:, 0, :, 0], D // H), ALU.mult)
                    link(nc.vector.tensor_tensor(given[:, D:FZ], before[:, D:FZ], factors[:, 0, :, 0], ALU.mult))
                    v.wait_ge(s["rows_used"][b], t + 2)
                    link(nc.vector.tensor_tensor(V[:, 0:FZ, 0], V[:, 0:FZ, 0], given[:], ALU.add))
                    v.wait_ge(s["factors_wide"], chunk + 1)
                    nc.vector.tensor_tensor_scan(V[:, 0:FZ, :].rearrange("p f k -> p (f k)"), flat(factors_w[:]),
                                                 V[:, 0:FZ, :].rearrange("p f k -> p (f k)"), 0.0,
                                                 ALU.mult, ALU.add).then_inc(s["states_done"], 1)
                    v.wait_ge(s["states_done"], chunk + 1)
                    assert link.n == LINKS, (kind, update, link.n)
            nc.vector.tensor_copy(g.tail[:, 0:R], values[:, 1, :, K - 1]).then_inc(s["tail_saved"], 1)
            v.wait_ge(s["tail_saved"], 1)


NG = 7
GC = C // NG
TURNS = ((0, 4), (4, GC))
assert C == NG * GC and GC <= 8


def nodes(nc, g, kind, rows=None, bias=None, gelu=False, renew=False, w_o=None, h_norm=None, copy=None,
          store=None,
          width=D, weights=None, from_sbuf=False, extra=False, out_w=0, out=None, tables=(),
          spread=None, seed=None):
    H = NH if kind == "multi" else 1
    FZ = D + H
    R = FZ + H
    states = g.d_e72 if kind == "multi" else g.d_e66
    st = g.node_state(R)
    gat, multi, summing = kind == "gat", kind == "multi", kind == "sum"
    norm = renew or not gat
    norms = 2 if store is not None else 1
    mix = multi or summing
    mix_in = D + 1 if summing else D
    PARTS, BUFS = 2 * REP, 4
    if mix:
        order = [("mix", 0)]
        for j in range(NG):
            order += ([("mix", j + 1)] if j + 1 < NG else []) + [("project", j)]
    else:
        order = [("project", j) for j in range(NG)]
    if not out_w:
        order = [o for o in order if o[0] == "mix"]
    place = {o: i for i, o in enumerate(order)}
    per = 512 // out_w if out_w else GC
    banks = [(k, min(k + per, GC)) for k in range(0, GC, per)]
    NB = len(banks)
    kin = width + (1 if extra else 0)
    groups = [(j * GC, (j + 1) * GC) for j in range(NG)]
    loads = [x for x in (w_o, h_norm, bias, None if from_sbuf else weights) if x is not None]
    with phase(nc, "dve_link turned_tails scanned tails_exp back_turned boundary written loaded ones_set shifted "
                   "exp_done summed gelu_done mixed activated var_ready rooted normed turned turn_copied stored multiplied "
                   "result_copied tabled spread_done seeded " + " ".join(f"collected{j}" for j in range(NG))) as s:
        wide = s.sbuf("wide", [P, FZ])
        mx = s.sbuf("mx", [FZ, P + 1])
        sm = s.sbuf("sm", [FZ, P + 1])
        fac = s.sbuf("fac", [FZ, 2, P])
        edge_state = s.sbuf("edge_state", [P, R])
        given = s.sbuf("given", [P, 2, FZ])
        fac2 = s.sbuf("fac2", [P, 2, FZ])
        both = s.sbuf("both", [P, FZ])
        merged = s.sbuf("merged", [P, R])
        bias_sb = s.sbuf("bias", [P, D])
        gs = s.sbuf("gs", [P, 2, D])
        w_o_sb = s.sbuf("w_o_sb", [mix_in, D])
        w_sb = s.sbuf("w_sb", [kin, max(out_w, 1)])
        agg_T = s.sbuf("agg_T", [mix_in, C if mix else 1, P])
        part = s.sbuf("part", [P, BUFS if summing else 1, 2, REP, GC * D])
        rows_T = s.sbuf("rows_T", [kin, C if out_w else 1, P])
        agg = s.sbuf("agg", [P, C, D])
        ls = s.sbuf("ls", [P, 3, GC])
        share = s.sbuf("share", [P, 2, GC])
        rec = s.sbuf("rec", [P, GC, H])
        own = s.sbuf("own", [P, GC, D])
        tmp = s.sbuf("tmp", [P, GC, D])
        stat = s.sbuf("stat", [P, 2, GC])
        if out is None and out_w:
            out = s.sbuf("out", [P, C, out_w])
        ps_tails = s.psum("ps_tails", [P, 512])
        ps_turn0 = s.psum("ps_turn0", [P, 512])
        ps_turn1 = s.psum("ps_turn1", [P, 512])
        ps_mix = s.psum("ps_mix", [P, 512])
        ps_out = s.psum("ps_out", [P, NB, 512])
        ps_turn = (ps_turn0, ps_turn1)
        ps_t, ps_b = ps_tails[:, 0:2 * P], ps_tails[:, 2 * P:2 * P + 2 * FZ]
        fresh = rows[:, :, width - D:width] if gat and not renew else agg
        block = s.block()

        def widen(v, link, src, out):
            nc.vector.tensor_copy(out[:, 0:D].rearrange("p (h d) -> p h d", h=H), bc(src, D // H))
            link(nc.vector.tensor_copy(out[:, D:FZ], src))

        @block.sync
        def _(sp):
            for src, dst in ((w_o, w_o_sb), (None if from_sbuf else weights, w_sb)):
                if src is not None:
                    sp.dma_start(dst[:], src).then_inc(s["loaded"], 16)
            for src, dst in ((h_norm, gs), (bias, bias_sb)):
                if src is not None:
                    sp.dma_start(dst[:], src.partition_broadcast(P)).then_inc(s["loaded"], 16)

            def load_sums(j):
                for ty in range(2):
                    for r in range(REP):
                        sums = table_rows(g.d_acc[r][ty * NP:(ty + 1) * NP, :])[:, slice(*groups[j]), :]
                        sp.dma_start(part[:, j % BUFS, ty, r, :].rearrange("p (c f) -> p c f", f=D),
                                     sums).then_inc(s[f"collected{j}"], 16)

            if summing:
                for j in range(BUFS):
                    load_sums(j)
            for j, (c0, c1) in enumerate(groups if store is not None else ()):
                sp.wait_ge(s["normed"], 2 * j + 2)
                sp.dma_start(node_rows(store)[:, c0:c1, :], g.x[:, c0:c1, :]).then_inc(s["stored"], 16)
            if store is not None:
                sp.wait_ge(s["stored"], 16 * NG)
            for j, (c0, c1) in enumerate(groups if out_w else ()):
                sp.wait_ge(s["result_copied"], NB * (j + 1))
                if summing and j + BUFS < NG:
                    load_sums(j + BUFS)
                for d, f0, f1 in tables:
                    sp.dma_start(table_rows(d)[:, c0:c1, :], out[:, c0:c1, f0:f1]).then_inc(s["tabled"], 16)
            if out_w:
                sp.wait_ge(s["tabled"], 16 * len(tables) * NG)
            if loads:
                sp.wait_ge(s["loaded"], 16 * len(loads))

        @block.vector
        def _(v):
            link = Link(v, s["dve_link"])
            def join():
                widen(v, link, g.tail[:, FZ:R], wide)
                nc.vector.memset(mx[:, 0:1], -BIG)
                link(nc.vector.memset(sm[:, 0:1], 0.0))
                v.wait_ge(s["turned_tails"], 1)
                link(nc.vector.tensor_tensor_scan(mx[:, 1:], g.pass_cut[0:FZ, :], ps_t[0:FZ, P:2 * P], mx[:, 0:1],
                                                  ALU.add, ALU.max))
                nc.vector.tensor_tensor(fac[:, 1], ps_t[0:FZ, P:2 * P], mx[:, 1:], ALU.subtract)
                link(nc.vector.tensor_tensor(fac[:, 0], mx[:, 0:P], g.pass_cut[0:FZ, :], ALU.add))
                nc.vector.tensor_tensor(fac[:, 0], fac[:, 0], mx[:, 1:], ALU.subtract).then_inc(s["scanned"], 1)
                v.wait_ge(s["tails_exp"], 1)
                link(nc.vector.tensor_tensor(fac[:, 1], fac[:, 1], ps_t[0:FZ, 0:P], ALU.mult))
                nc.vector.tensor_tensor_scan(sm[:, 1:], fac[:, 0], fac[:, 1], sm[:, 0:1], ALU.mult, ALU.add).then_inc(s["scanned"], 1)
                v.wait_ge(s["back_turned"], 1)
                link(nc.vector.tensor_copy(flat(given[:]), ps_b))
                v.wait_ge(s["boundary"], 16)
                widen(v, link, edge_state[:, FZ:R], wide)
                link(nc.vector.tensor_tensor(both[:], wide[:], given[:, 1], ALU.max))
                nc.vector.tensor_tensor(fac2[:, 0], wide[:], both[:], ALU.subtract)
                nc.vector.tensor_tensor(fac2[:, 1], given[:, 1], both[:], ALU.subtract).then_inc(s["scanned"], 1)
                v.wait_ge(s["tails_exp"], 2)
                nc.vector.tensor_tensor(fac2[:, 0], fac2[:, 0], edge_state[:, 0:FZ], ALU.mult)
                link(nc.vector.tensor_tensor(fac2[:, 1], fac2[:, 1], given[:, 0], ALU.mult))
                nc.vector.tensor_tensor(merged[:, 0:FZ], fac2[:, 0], fac2[:, 1], ALU.add)
                nc.vector.tensor_copy(merged[:, FZ:R], both[:, D:FZ]).then_inc(s["scanned"], 1)

            if not summing:
                join()
            if extra:
                nc.vector.memset(rows_T[width:width + 1, :, :], 1.0).then_inc(s["ones_set"], 1)
            if width > D:
                link(nc.vector.tensor_copy(rows[:, :, 0:D], g.x[:]))
            if loads:
                v.wait_ge(s["loaded"], 16 * len(loads))

            def finish(j):
                cols = slice(*groups[j])
                v.wait_ge(s[f"collected{j}"], 16 * (PARTS if summing else GC))
                if summing:
                    sums = part[:, j % BUFS]
                    link(nc.vector.tensor_tensor(sums[:, :, 0:2], sums[:, :, 0:2], sums[:, :, 2:4], ALU.add))
                    link(nc.vector.tensor_tensor(sums[:, :, 0], sums[:, :, 0], sums[:, :, 1], ALU.add))
                    for ty in range(2):
                        by_node = sums[:, ty, 0].rearrange("p (c f) -> p c f", f=D)
                        last = nc.vector.tensor_tensor(by_node, by_node, bc(g.attention[:, ty, cols], D), ALU.mult)
                    link(last)
                    nc.vector.tensor_tensor(agg[:, cols, :].rearrange("p c f -> p (c f)"), sums[:, 0, 0],
                                            sums[:, 1, 0], ALU.add).then_inc(s["summed"], 1)
                    return
                if not gat:
                    if j:
                        v.wait_ge(s["summed"], j)
                    link(nc.vector.tensor_scalar(rec[:], st[:, cols, D:D + H], 1e-9, None, ALU.add))
                    link(nc.vector.reciprocal(rec[:], rec[:]))
                    for h in range(H):
                        w = D // H
                        last = nc.vector.tensor_tensor(agg[:, cols, h * w:(h + 1) * w],
                                                       st[:, cols, h * w:(h + 1) * w], bc(rec[:, :, h], w), ALU.mult)
                    last.then_inc(s["summed"], 1)
                    return
                h, m, z = g.proj, st[:, cols, 65], st[:, cols, 64]
                link(nc.vector.tensor_tensor(ls[:, 0], h[:, cols, 64], h[:, cols, 65], ALU.add))
                link(nc.vector.scalar_tensor_tensor(ls[:, 0], ls[:, 0], 0.2, ls[:, 0], ALU.mult, ALU.max))
                link(nc.vector.tensor_tensor(ls[:, 1], ls[:, 0], m, ALU.max))
                nc.vector.tensor_tensor(share[:, 0], m, ls[:, 1], ALU.subtract)
                nc.vector.tensor_tensor(share[:, 1], ls[:, 0], ls[:, 1], ALU.subtract).then_inc(s["shifted"], 1)
                v.wait_ge(s["exp_done"], j + 1)
                link(nc.vector.tensor_tensor(ls[:, 2], z, share[:, 0], ALU.mult))
                link(nc.vector.tensor_tensor(ls[:, 2], ls[:, 2], share[:, 1], ALU.add))
                link(nc.vector.reciprocal(ls[:, 2], ls[:, 2]))
                link(nc.vector.tensor_tensor(share[:], share[:], mid(ls[:, 2], 2), ALU.mult))
                nc.vector.tensor_tensor(own[:], h[:, cols, 0:D], bc(share[:, 1], D), ALU.mult)
                link(nc.vector.tensor_tensor(tmp[:], st[:, cols, 0:D], bc(share[:, 0], D), ALU.mult))
                link(nc.vector.tensor_tensor(own[:], own[:], tmp[:], ALU.add))
                nc.vector.tensor_tensor(fresh[:, cols, :], own[:], mid(bias_sb[:], GC), ALU.add).then_inc(s["summed"], 1)

            def normalise(j, n=0):
                cols = slice(*groups[j])
                target = (g.h if multi and n == 0 else g.x)[:, cols, :]
                if n:
                    v.wait_ge(s["normed"], norms * j + n)
                    add = g.h[:, cols, :]
                elif summing:
                    v.wait_ge(s["activated"], j + 1)
                    add = agg[:, cols, :]
                elif multi:
                    v.wait_ge(s["mixed"], j + 1)
                    add = ps_mix[:, 0:GC * D].rearrange("p (c f) -> p c f", f=D)
                else:
                    v.wait_ge(s["summed"], j + 1)
                    add = fresh[:, cols, :]
                link(nc.vector.tensor_tensor(target, target, add, ALU.add))
                link(nc.vector.tensor_reduce(stat[:, 0], target, AX.X, ALU.add))
                link(nc.vector.scalar_tensor_tensor(target, bc(stat[:, 0], D), -1.0 / D, target, ALU.mult, ALU.add))
                link(nc.vector.tensor_tensor(tmp[:], target, target, ALU.mult))
                link(nc.vector.tensor_reduce(stat[:, 1], tmp[:], AX.X, ALU.add))
                nc.vector.tensor_scalar(stat[:, 1], stat[:, 1], 1.0 / D, 1e-5, ALU.mult, ALU.add).then_inc(s["var_ready"], 1)
                v.wait_ge(s["rooted"], norms * j + n + 1)
                link(nc.vector.reciprocal(stat[:, 1], stat[:, 1]))
                last = nc.vector.tensor_tensor(target, target, bc(stat[:, 1], D), ALU.mult)
                if multi and n == 0:
                    link(last)
                    link(nc.vector.tensor_tensor(target, target, mid(gs[:, 0], GC), ALU.mult))
                    last = nc.vector.tensor_tensor(target, target, mid(gs[:, 1], GC), ALU.add)
                last.then_inc(s["normed"], 1)
                if copy is not None:
                    v.wait_ge(s["normed"], j + 1)
                    link(nc.vector.tensor_copy(copy[:, cols, :], target))

            finish(0)
            for j in range(NG):
                if mix and j + 1 < NG:
                    finish(j + 1)
                if norm:
                    for n in range(norms):
                        normalise(j, n)
                if not mix and j + 1 < NG:
                    finish(j + 1)

        def turned_rows(step, j):
            return (agg, agg_T, D) if step == "mix" else (rows, rows_T, width)

        @block.scalar
        def _(act):
            if not summing:
                act.wait_ge(s["scanned"], 1)
                nc.scalar.activation(flat(fac[:]), flat(fac[:]), ACT.Exp).then_inc(s["tails_exp"], 1)
                act.wait_ge(s["scanned"], 3)
                nc.scalar.activation(flat(fac2[:]), flat(fac2[:]), ACT.Exp).then_inc(s["tails_exp"], 1)

            def functions(j):
                cols = slice(*groups[j])
                if gat:
                    act.wait_ge(s["shifted"], j + 1)
                    nc.scalar.activation(flat(share[:]), flat(share[:]), ACT.Exp).then_inc(s["exp_done"], 1)
                if gelu:
                    act.wait_ge(s["summed"], j + 1)
                    nc.scalar.activation(fresh[:, cols, :], fresh[:, cols, :], ACT.Gelu).then_inc(s["gelu_done"], 1)
                for n in range(norms if norm else 0):
                    act.wait_ge(s["var_ready"], norms * j + n + 1)
                    nc.scalar.activation(stat[:, 1], stat[:, 1], ACT.Sqrt).then_inc(s["rooted"], 1)

            def copy_turned(step, j):
                _, turned_T, w = turned_rows(step, j)
                for i, (k0, k1) in enumerate(TURNS):
                    act.wait_ge(s["turned"], 2 * place[step, j] + i + 1)
                    nc.scalar.copy(flat(turned_T[0:w, j * GC + k0:j * GC + k1, :]),
                                   ps_turn[i][0:w, 0:(k1 - k0) * P]).then_inc(s["turn_copied"], 1)

            if mix:
                copy_turned("mix", 0)
            for j in range(NG):
                if summing:
                    act.wait_ge(s["mixed"], j + 1)
                    nc.scalar.activation(agg[:, slice(*groups[j]), :].rearrange("p c f -> p (c f)"),
                                         ps_mix[:, 0:GC * D], ACT.Tanh).then_inc(s["activated"], 1)
                if mix and j + 1 < NG:
                    copy_turned("mix", j + 1)
                functions(j)
                if out_w:
                    copy_turned("project", j)
                    for k, (k0, k1) in enumerate(banks):
                        act.wait_ge(s["multiplied"], NB * j + k + 1)
                        nc.scalar.copy(out[:, j * GC + k0:j * GC + k1, 0:out_w],
                                       ps_out[:, k, 0:(k1 - k0) * out_w].rearrange("p (c w) -> p c w", w=out_w)
                                       ).then_inc(s["result_copied"], 1)

        @block.tensor
        def _(pe):
            if not summing:
                pe.wait_ge(s["dve_link"], 1)
                nc.tensor.transpose(ps_t[0:FZ, 0:P], g.tail[:, 0:FZ], g.ident[:])
                nc.tensor.transpose(ps_t[0:FZ, P:2 * P], wide[:], g.ident[:]).then_inc(s["turned_tails"], 1)
                pe.wait_ge(s["scanned"], 2)
                nc.tensor.transpose(ps_b[:, 0:FZ], sm[:, 0:P], g.ident[0:FZ, 0:FZ])
                nc.tensor.transpose(ps_b[:, FZ:2 * FZ], mx[:, 0:P], g.ident[0:FZ, 0:FZ]).then_inc(s["back_turned"], 1)
            if loads:
                pe.wait_ge(s["loaded"], 16 * len(loads))
            if extra or summing:
                pe.wait_ge(s["ones_set"], 1)
            for p, (step, j) in enumerate(order):
                src, src_T, w = turned_rows(step, j)
                ready = "summed" if step == "mix" else "normed" if norm else "gelu_done"
                pe.wait_ge(s[ready], j + 1)
                for i, (k0, k1) in enumerate(TURNS):
                    if p:
                        pe.wait_ge(s["turn_copied"], 2 * p - 1 + i)
                    for k in range(k0, k1):
                        mm = nc.tensor.transpose(ps_turn[i][0:w, (k - k0) * P:(k - k0 + 1) * P],
                                                 src[:, j * GC + k, :], g.ident[:])
                    mm.then_inc(s["turned"], 1)
                pe.wait_ge(s["turn_copied"], 2 * p + 2)
                if step == "mix":
                    if j and summing:
                        pe.wait_ge(s["activated"], j)
                    elif j:
                        pe.wait_ge(s["var_ready"], norms * (j - 1) + 1)
                    for k in range(GC):
                        mm = nc.tensor.matmul(ps_mix[:, k * D:(k + 1) * D], agg_T[:, j * GC + k, :], w_o_sb[:],
                                              start=True, stop=True)
                    mm.then_inc(s["mixed"], 1)
                else:
                    for n, (k0, k1) in enumerate(banks):
                        if j:
                            pe.wait_ge(s["result_copied"], NB * (j - 1) + n + 1)
                        for k in range(k0, k1):
                            mm = nc.tensor.matmul(ps_out[:, n, (k - k0) * out_w:(k - k0 + 1) * out_w],
                                                  rows_T[:, j * GC + k, :], weights if from_sbuf else w_sb[:],
                                                  start=True, stop=True)
                        mm.then_inc(s["multiplied"], 1)

        @block.gpsimd
        def _(gp):
            if summing:
                nc.gpsimd.memset(agg_T[D:mix_in, :, :], 1.0).then_inc(s["ones_set"], 1)
            else:
                gp.indirect_dma_start(edge_state[:], None, states[:, :], offset(g.idx_join[:])).then_inc(s["boundary"], 16)
                gp.wait_ge(s["boundary"], 16)
                gp.wait_ge(s["scanned"], 4)
                gp.indirect_dma_start(states[:, :], offset(g.idx_join[:]), merged[:], None).then_inc(s["written"], 16)
                gp.wait_ge(s["written"], 16)
            for j, (c0, c1) in enumerate(groups if not summing else ()):
                for c in range(c0, c1):
                    gp.indirect_dma_start(st[:, c, :], None, states[:, :],
                                          offset(g.idx_last[:, c:c + 1])).then_inc(s[f"collected{j}"], 16)
            if out_w:
                d, f0, f1 = spread
                for j, (c0, c1) in enumerate(groups):
                    gp.wait_ge(s["result_copied"], NB * (j + 1))
                    for c in range(c0, c1):
                        gp.indirect_dma_start(d[:, :], offset(g.idx_first[:, c:c + 1]),
                                              out[:, c, f0:f1], None).then_inc(s["spread_done"], 16)
                gp.wait_ge(s["tabled"], 16 * len(tables) * NG)
                gp.indirect_dma_start(g.seed[:, 0:seed[1]], None, seed[0][:, :],
                                      offset(g.dst0[:])).then_inc(s["seeded"], 16)
                gp.wait_ge(s["spread_done"], 16 * C)
                gp.wait_ge(s["seeded"], 16)


class Graph:

    def node_state(self, width):
        return self.states_sb[:, :, 0:width]


def build(nc, a, out):
    g = Graph()
    with ExitStack() as ctx:
        def sb(name, shape, dt=F32):
            return ctx.enter_context(nc.sbuf_tensor(name, shape, dt))

        def dram(name, shape, dt=F32):
            return nc.dram_tensor(name, shape, dt, kind="Internal").ap()

        g.x, g.h = sb("x", [P, C, D]), sb("h", [P, C, D])
        g.states_sb = sb("states_sb", [P, C, 72])
        g.ident, g.ones, g.iota = sb("ident", [P, P]), sb("ones", [P, P]), sb("iota", [P, P])
        g.before, g.after = sb("before", [P, P]), sb("after", [P, P])
        g.pcol = sb("pcol", [P, 1])
        g.same, g.cut = sb("same", [P, KT + 2 * K]), sb("cut", [P, KT])
        g.src = sb("src", [P, KT + 2 * K], I32)
        g.key = sb("key", [P, KT])
        g.attention = sb("attention", [P, 2, C])
        g.pass_cut = sb("pass_cut", [68, P])
        g.dst0_x = sb("dst0_x", [P, 1], I32)
        g.dst0, g.idx_join = sb("dst0", [P, 1], I32), sb("idx_join", [P, 1], I32)
        g.idx_first, g.idx_last = sb("idx_first", [P, C], I32), sb("idx_last", [P, C], I32)
        g.seed, g.tail = sb("seed", [P, 96]), sb("tail", [P, 72])
        g.gat_w = sb("gat_w", [P, 2, D + 2])
        g.d_x = a["x_pad"]
        g.d_acc = [dram(f"d_acc{r}", [ACC_ROWS, D]) for r in range(REP)]
        g.d_b1, g.d_b64, g.d_b96 = (dram(f"d_b{w}", [B_ROWS, w]) for w in (1, 64, 96))
        g.d_e66, g.d_e72 = (dram(f"d_e{w}", [E_ROWS, w]) for w in (66, 72))
        g.d_t66, g.d_t128, g.d_t160 = (dram(f"d_t{w}", [NP, w]) for w in (66, 128, 160))
        g.d_q64, g.d_q96 = dram("d_q64", [NP, 64]), dram("d_q96", [NP, 96])
        g.d_edge = dram("d_edge", [EP, DE])


        prepare(nc, g, a)
        layer0_edges(nc, g, a)

        with scratch(nc, "proj", [P, C, D + 2]) as proj:
            g.proj = proj
            gat = dict(out=proj, out_w=D + 2, from_sbuf=True, tables=[(g.d_t66, 0, D + 2)],
                       spread=(g.d_b1, D + 1, D + 2), seed=(g.d_t66, D + 2))
            std = dict(gat, weights=g.gat_w[0:D, 1, :])
            nodes(nc, g, "sum", g.x, w_o=a["l0_w"], **std)
            with nc.Fori(0, 3):
                edges(nc, g, "gat")
                nodes(nc, g, "gat", g.h, bias=a["b_std"], gelu=True, **std)
            edges(nc, g, "gat", clear=g.d_b96)
            with scratch(nc, "stacked", [P, C, 2 * D]) as stacked:
                nodes(nc, g, "gat", stacked, bias=a["b_std"], gelu=True, width=2 * D,
                      **dict(gat, weights=g.gat_w[:, 0, :]))
            edges(nc, g, "gat")
            nodes(nc, g, "gat", g.x, bias=a["b_skip"], renew=True, weights=a["l2_w"], extra=True, out_w=3 * D,
                  tables=[(g.d_t128, 0, 2 * D), (g.d_q64, 2 * D, 3 * D)], spread=(g.d_b64, 2 * D, 3 * D),
                  seed=(g.d_q64, D))
        edges(nc, g, "dot", a)

        nodes(nc, g, "dot", g.x, copy=g.h, weights=a["l3_w0"], extra=True, out_w=192,
              tables=[(g.d_t128, 0, 128), (g.d_q64, 128, 192)], spread=(g.d_b64, 128, 192), seed=(g.d_q64, D))
        def w_edges(i):
            return {k: a[k][i] for k in ("w_e", "w_em", "e_norm")}

        edges(nc, g, "multi", w_edges(0))
        with nc.Fori(0, 2) as i:
            nodes(nc, g, "multi", g.h, w_o=a["w_o"][i], h_norm=a["h_norm"][i], weights=a["l3_w"][i + 1], extra=True,
                  out_w=256, tables=[(g.d_t160, 0, 160), (g.d_q96, 160, 256)], spread=(g.d_b96, 160, 256),
                  seed=(g.d_q96, 96))
            edges(nc, g, "multi", w_edges(i + 1), True)
        nodes(nc, g, "multi", w_o=a["w_o"][2], h_norm=a["h_norm"][2], store=out)


_OUT = ((N, D), "float32")


def lay_out(x, src, dst, edge_attr_32, edge_type_2, L0_gnn_relation_emb, L0_gnn_att_w, L0_gnn_att_b, L0_gnn_W_w,
            L0_gnn_W_b, L1_gnn_W_std, L1_gnn_a_src_std, L1_gnn_a_dst_std, L1_gnn_b_std, L1_gnn_W_skip,
            L1_gnn_a_src_skip, L1_gnn_a_dst_skip, L1_gnn_b_skip, L2_gnn_Wq, L2_gnn_bq, L2_gnn_Wk, L2_gnn_bk,
            L2_gnn_Wf, L2_gnn_bf, L3_gnn_Wq, L3_gnn_Wk, L3_gnn_Wv, L3_gnn_Wo, L3_gnn_We, L3_gnn_Wem, L3_gnn_bem,
            L3_gnn_gn, L3_gnn_bn, L3_gnn_ge, L3_gnn_be):
    def padded(v, shape, fill=0):
        out = np.full(shape, fill, v.dtype)
        out[tuple(slice(0, n) for n in v.shape)] = v
        return out

    ids = np.full(EP + 2, NP - 1, np.int32)
    ids[0] = -1
    ids[1:E + 1] = dst
    f = np.float32
    L = L3_gnn_Wq.shape[0]
    l3_w = np.zeros((L, D + 1, 256), f)
    w_em = np.zeros((L, P, P), f)
    e_norm = np.zeros((L, 2, DE), f)
    w_e = np.zeros((L, P, 16), f)
    for i in range(L):
        l3_w[i, 0:D, 32:96], l3_w[i, 0:D, 96:160], l3_w[i, 0:D, 160:224] = L3_gnn_Wk[i], L3_gnn_Wv[i], L3_gnn_Wq[i]
        for q in range(4):
            w_e[i, 32 * q:32 * q + 32, 4 * q:4 * q + 4] = L3_gnn_We[i]
        if i:
            l3_w[i, 0:D, 0:32], l3_w[i, 0:D, 224:256] = L3_gnn_Wem[i - 1, 0:D], L3_gnn_Wem[i - 1, D:2 * D]
            l3_w[i, D, 224:256] = L3_gnn_bem[i - 1]
            e_norm[i, 0], e_norm[i, 1] = L3_gnn_ge[i - 1], L3_gnn_be[i - 1]
            for q in range(4):
                w_em[i, 32 * q:32 * q + 32, 32 * q:32 * q + 32] = L3_gnn_Wem[i - 1, 2 * D:]
    l3_w0 = np.zeros((D + 1, 192), f)
    l3_w0[0:D] = l3_w[0, 0:D, 32:224]
    l2_w = np.zeros((D + 1, 192), f)
    for j, (w, b) in enumerate(((L2_gnn_Wk, L2_gnn_bk), (L2_gnn_Wf, L2_gnn_bf), (L2_gnn_Wq, L2_gnn_bq))):
        l2_w[0:D, 64 * j:64 * j + 64], l2_w[D, 64 * j:64 * j + 64] = w, b
    return {
        "x_pad": padded(x, (NP, D)),
        "dst_ext": np.stack([ids[p * KT:p * KT + KT + 2] for p in range(P)]),
        "src_pad": padded(src, (EP,), NP - 1).reshape(P, KT),
        "type_pad": padded(edge_type_2, (EP,)).reshape(P, KT),
        "edge_pad": padded(edge_attr_32, (EP, DE)),
        "rel_rows": np.concatenate([L0_gnn_att_w.reshape(2, D), L0_gnn_relation_emb]),
        "att_b": L0_gnn_att_b,
        "l0_w": np.concatenate([L0_gnn_W_w.T, L0_gnn_W_b[None]]),
        "gat_w_skip": L1_gnn_W_skip, "gat_w_std": L1_gnn_W_std,
        "gat_wT": np.concatenate([L1_gnn_W_skip.T, L1_gnn_W_std.T], 1),
        "gat_a": np.stack([L1_gnn_a_src_skip, L1_gnn_a_dst_skip, L1_gnn_a_src_std, L1_gnn_a_dst_std], 1),
        "b_std": L1_gnn_b_std, "b_skip": L1_gnn_b_skip,
        "l2_w": l2_w, "l3_w0": l3_w0, "l3_w": l3_w, "w_e": w_e, "w_em": w_em, "e_norm": e_norm,
        "w_o": L3_gnn_Wo, "h_norm": np.stack([L3_gnn_gn, L3_gnn_bn], 1),
    }


def kernel(**inputs):
    import concourse.bacc as bacc
    from concourse.bass_utils import run_bass_kernel_spmd

    laid = {k: np.ascontiguousarray(v) for k, v in lay_out(**{k: np.asarray(v) for k, v in inputs.items()}).items()}
    nc = bacc.Bacc("TRN2", target_bir_lowering=False, num_devices=1)
    aps = {k: nc.dram_tensor(f"in_{k}", v.shape, mybir.dt.from_np(v.dtype), kind="ExternalInput").ap()
           for k, v in laid.items()}
    out = nc.dram_tensor("out_0", (NP, D), F32, kind="ExternalOutput").ap()
    build(nc, aps, out)
    r = run_bass_kernel_spmd(nc, [{f"in_{k}": v for k, v in laid.items()}], core_ids=[0])
    return np.ascontiguousarray(r.results[0]["out_0"][0:N])
```
